# Optimizing a Trainium2 kernel written in Bass

```python
import numpy as np
import jax
import jax.numpy as jnp

def _softmax(x, axis=-1):
    return jax.nn.softmax(x, axis=axis)

def _gelu(x):
    return jax.nn.gelu(x, approximate=True)

def _silu(x):
    return jax.nn.silu(x)

def _sigmoid(x):
    return jax.nn.sigmoid(x)

def _layernorm(x, axis=-1, eps=1e-05):
    m = jnp.mean(x, axis=axis, keepdims=True)
    v = jnp.var(x, axis=axis, keepdims=True)
    return (x - m) / jnp.sqrt(v + eps)

def _scatter_add(tgt, idx, src, axis=0):
    return tgt.at[idx].add(src)

def _segment_sum(src, seg, n):
    return jax.ops.segment_sum(src, seg, n)
kernel_name = 'mk_xattn_ffn_d2_seqx_r8_95edbe'

def setup_inputs(seed: int=0):
    np.random.seed(seed)
    _w = jnp.asarray

    def _rec_inputs():
        import jax
        import jax.numpy as jnp
        _rk = jax.random.key(seed)
        x = 4.136e-05 + 0.9999 * jax.random.normal(jax.random.fold_in(_rk, 1), (64, 128, 128), jnp.float32)
        _lenS = 128 - jax.random.randint(jax.random.fold_in(_rk, 7), (64,), 0, max(1, 128 // 4) + 1, jnp.int32)
        _lenS2 = 77 - jax.random.randint(jax.random.fold_in(_rk, 8), (64,), 0, max(1, 77 // 4) + 1, jnp.int32)
        _ctx_2048P = jax.random.normal(jax.random.fold_in(_rk, 11), (64, 16, 256), jnp.float32)
        _ctx_2048c = jax.random.dirichlet(jax.random.fold_in(_rk, 511), 0.3 * jnp.ones((16,), jnp.float32), (64, 77))
        _ctx_2048t = jnp.einsum('bsk,bkd->bsd', _ctx_2048c, _ctx_2048P)
        _ctx_2048t = _ctx_2048t * jax.lax.rsqrt(jnp.mean(jnp.square(_ctx_2048t)) + 1e-12) * 0.953939
        ctx_2048 = -0.000392918 + 0.999932 * (_ctx_2048t + 0.3 * jax.random.normal(jax.random.fold_in(_rk, 611), (64, 77, 256), jnp.float32))
        _validS = jnp.arange(128)[None, :] < _lenS[:, None]
        _validS2 = jnp.arange(77)[None, :] < _lenS2[:, None]
        _causal = jnp.tril(jnp.ones((128, 128), dtype=bool))
        mask_BxS2_ik0 = jnp.where(jnp.broadcast_to(_validS2[:, :], (64, 77)), 0, 1).astype(jnp.int32)
        mask_BxS2_if0 = jnp.where(jnp.ones((64, 77), dtype=bool), 4, 0).astype(jnp.int32)
        return (x, ctx_2048, mask_BxS2_ik0, mask_BxS2_if0)
    x, ctx_2048, mask_BxS2_ik0, mask_BxS2_if0 = _rec_inputs()

    def _L0_xattn_setup():
        import jax, jax.numpy as jnp
        import numpy as np
        UNITS = 128
        NUM_HEADS = 8

        def _split_heads(x, n):
            B, S, D = x.shape
            return x.reshape(B, S, n, D // n).transpose(0, 2, 1, 3)
        key = jax.random.key(seed)
        k1, k2, k3 = jax.random.split(key, 3)
        B, S = (8, 128)
        memory = jax.random.normal(k1, (B, S, 2 * UNITS), dtype=jnp.float32)
        query = jax.random.normal(k2, (B, S, UNITS), dtype=jnp.float32)
        seq_mask = jax.random.randint(k3, (B, S), 0, 2, dtype=jnp.int32)
        b = jnp.zeros((1,), dtype=jnp.float32)
        return {'memory': memory, 'query': query, 'seq_mask': seq_mask, 'b': b}
    _L0_xattn_all = _L0_xattn_setup()
    _L0_xattn_in = {k: v for k, v in _L0_xattn_all.items() if k in ('b',)}
    del _L0_xattn_all

    def _L0_ffn_setup():
        import jax, jax.numpy as jnp
        import numpy as np
        import math
        D_IN = 128
        FEATURES = (512, 512, 128)
        BATCH, SEQ = (8, 256)

        def _conn_dense(kernel_bool, x):
            w = jnp.where(kernel_bool, jnp.float32(1.0), jnp.float32(-1.0))
            return x @ w
        key = jax.random.key(seed)
        kx, kk0, kk1, kk2 = jax.random.split(key, 4)
        x = jax.random.normal(kx, (BATCH, SEQ, D_IN), dtype=jnp.float32)
        k0 = jax.random.randint(kk0, (2 * D_IN, FEATURES[0]), 0, 2).astype(jnp.bool_)
        k1 = jax.random.randint(kk1, (FEATURES[0], FEATURES[1]), 0, 2).astype(jnp.bool_)
        k2 = jax.random.randint(kk2, (FEATURES[1], FEATURES[2]), 0, 2).astype(jnp.bool_)
        s0 = jnp.asarray(1.0 / math.sqrt(2 * D_IN), dtype=jnp.float32)
        s1 = jnp.asarray(1.0 / math.sqrt(FEATURES[0]), dtype=jnp.float32)
        s2 = jnp.asarray(1.0 / math.sqrt(FEATURES[1]), dtype=jnp.float32)
        return {'x': x, 'k0': k0, 'k1': k1, 'k2': k2, 's0': s0, 's1': s1, 's2': s2}
    _L0_ffn_all = _L0_ffn_setup()
    _L0_ffn_in = {k: v for k, v in _L0_ffn_all.items() if k in ('k0', 'k1', 'k2', 's0', 's1', 's2')}
    del _L0_ffn_all

    def _L1_xattn_setup():
        import jax, jax.numpy as jnp
        import numpy as np
        B, L, P = (4, 512, 128)
        D_MODEL = 128
        D_GLOBAL = 256
        HEADDIM = 32
        EPSILON = 0.001
        RMS_EPS = 1e-05

        def rmsnorm(x, g, eps=RMS_EPS):
            var = jnp.mean(jnp.square(x), axis=-1, keepdims=True)
            return x * jax.lax.rsqrt(var + eps) * g

        def _hnet_depool(h, h_patch_full, patch_lens):
            h_patch = h_patch_full[..., :D_MODEL]
            bsz, plen = (h_patch.shape[0], h_patch.shape[1])
            seqlen = h.shape[1]
            logp = jnp.full((bsz, plen), -EPSILON, dtype=jnp.float32)
            bidx = jnp.cumsum(patch_lens, axis=1) - 1
            boundary_mask = jnp.zeros((bsz, seqlen), dtype=jnp.int32)
            boundary_mask = boundary_mask.at[jnp.arange(bsz)[:, None], bidx].set(1)
            dt = (-jnp.log(-jnp.expm1(logp))).astype(h_patch.dtype)
            x = h_patch / dt[..., None]
            n_heads = D_MODEL // HEADDIM
            A = -jnp.ones((n_heads,), dtype=jnp.float32)
            bcoef = jnp.exp(logp).astype(h_patch.dtype)
            x4 = x.reshape(bsz, plen, n_heads, HEADDIM)
            a = jnp.exp(dt[:, :, None] * A[None, None, :])
            u = (dt * bcoef)[:, :, None, None] * x4
            a_b = jnp.broadcast_to(a[..., None], u.shape)

            def comb(lft, rgt):
                aL, uL = lft
                aR, uR = rgt
                return (aL * aR, uL * aR + uR)
            _, s = jax.lax.associative_scan(comb, (a_b, u), axis=1)
            depool = s.reshape(bsz, plen, D_MODEL)
            plug = jnp.clip(jnp.cumsum(boundary_mask, axis=1) - 1, 0, plen - 1)
            depool_out = depool[jnp.arange(bsz)[:, None], plug]
            return depool_out + h
        key = jax.random.key(seed)
        k1, k2, k3, k4 = jax.random.split(key, 4)
        embeds = jax.random.normal(k1, (B, L, D_MODEL), dtype=jnp.float32)
        patch_embeds = jax.random.normal(k2, (B, P, D_GLOBAL), dtype=jnp.float32)
        patch_lens = jnp.full((B, P), L // P, dtype=jnp.int64)
        W_in = jax.random.normal(k3, (D_MODEL, D_MODEL), dtype=jnp.float32) * 0.02
        b_in = jnp.zeros((D_MODEL,), dtype=jnp.float32)
        g_res = jnp.ones((D_MODEL,), dtype=jnp.float32)
        g_init = jnp.ones((D_GLOBAL,), dtype=jnp.float32)
        return {'embeds': embeds, 'patch_embeds': patch_embeds, 'patch_lens': patch_lens, 'W_in': W_in, 'b_in': b_in, 'g_res': g_res, 'g_init': g_init}
    _L1_xattn_all = _L1_xattn_setup()
    _L1_xattn_in = {k: v for k, v in _L1_xattn_all.items() if k in ('W_in', 'b_in', 'g_res', 'g_init')}
    del _L1_xattn_all

    def _L1_ffn_setup():
        import jax, jax.numpy as jnp
        import numpy as np
        K = 2
        TEMP = 1.0
        key = jax.random.key(seed)
        ks = jax.random.split(key, 5)
        B, S, D, O, E = (4, 256, 128, 128, 8)
        scale = 1.0 / np.sqrt(D)
        x = jax.random.normal(ks[0], (B, S, D), dtype=jnp.float32)
        W = jax.random.normal(ks[1], (E, O, D), dtype=jnp.float32) * scale
        b = jax.random.normal(ks[2], (E, O), dtype=jnp.float32) * 0.01
        Wg = jax.random.normal(ks[3], (E, D), dtype=jnp.float32) * scale
        bg = jnp.zeros((E,), dtype=jnp.float32)
        return {'x': x, 'W': W, 'b': b, 'Wg': Wg, 'bg': bg}
    _L1_ffn_all = _L1_ffn_setup()
    _L1_ffn_in = {k: v for k, v in _L1_ffn_all.items() if k in ('W', 'b', 'Wg', 'bg')}
    del _L1_ffn_all
    return {'x': x, 'ctx_2048': ctx_2048, 'mask_BxS2_ik0': mask_BxS2_ik0, 'mask_BxS2_if0': mask_BxS2_if0, 'L0_xattn_b': _L0_xattn_in['b'], 'L0_ffn_k0': _L0_ffn_in['k0'], 'L0_ffn_k1': _L0_ffn_in['k1'], 'L0_ffn_k2': _L0_ffn_in['k2'], 'L0_ffn_s0': _L0_ffn_in['s0'], 'L0_ffn_s1': _L0_ffn_in['s1'], 'L0_ffn_s2': _L0_ffn_in['s2'], 'L1_xattn_W_in': _L1_xattn_in['W_in'], 'L1_xattn_b_in': _L1_xattn_in['b_in'], 'L1_xattn_g_res': _L1_xattn_in['g_res'], 'L1_xattn_g_init': _L1_xattn_in['g_init'], 'L1_ffn_W': _L1_ffn_in['W'], 'L1_ffn_b': _L1_ffn_in['b'], 'L1_ffn_Wg': _L1_ffn_in['Wg'], 'L1_ffn_bg': _L1_ffn_in['bg']}

def reference(x, ctx_2048, mask_BxS2_ik0, mask_BxS2_if0, L0_xattn_b, L0_ffn_k0, L0_ffn_k1, L0_ffn_k2, L0_ffn_s0, L0_ffn_s1, L0_ffn_s2, L1_xattn_W_in, L1_xattn_b_in, L1_xattn_g_res, L1_xattn_g_init, L1_ffn_W, L1_ffn_b, L1_ffn_Wg, L1_ffn_bg):
    import jax
    import jax.numpy as jnp

    def _L0_xattn_ref(memory, query, seq_mask, b):
        import jax, jax.numpy as jnp
        import numpy as np
        UNITS = 128
        NUM_HEADS = 8

        def _split_heads(x, n):
            B, S, D = x.shape
            return x.reshape(B, S, n, D // n).transpose(0, 2, 1, 3)
        H = NUM_HEADS
        depth = UNITS // H
        Q = _split_heads(query, H) * depth ** (-0.5)
        k_mem, v_mem = jnp.split(memory, 2, axis=2)
        K = _split_heads(k_mem, H)
        V = _split_heads(v_mem, H)
        logits = jnp.einsum('bhqd,bhkd->bhqk', Q, K) + b[0]
        mask = seq_mask.astype(jnp.float32)[:, None, None, :]
        logits = logits + -1e+30 * (1.0 - mask)
        weights = jax.nn.softmax(logits, axis=-1)
        out = jnp.einsum('bhqk,bhkd->bhqd', weights, V)
        B, _, S, _ = out.shape
        return out.transpose(0, 2, 1, 3).reshape(B, S, UNITS)

    def _L0_ffn_ref(x, k0, k1, k2, s0, s1, s2):
        import jax, jax.numpy as jnp
        import numpy as np
        import math
        D_IN = 128
        FEATURES = (512, 512, 128)
        BATCH, SEQ = (8, 256)

        def _conn_dense(kernel_bool, x):
            w = jnp.where(kernel_bool, jnp.float32(1.0), jnp.float32(-1.0))
            return x @ w
        h = jnp.concatenate([x, -x], axis=-1)
        h = s0 * _conn_dense(k0, h)
        h = jax.nn.relu(h) * 2
        h = s1 * _conn_dense(k1, h)
        h = jax.nn.relu(h) * 2
        h = s2 * _conn_dense(k2, h)
        return h

    def _L1_xattn_ref(embeds, patch_embeds, patch_lens, W_in, b_in, g_res, g_init):
        import jax, jax.numpy as jnp
        import numpy as np
        B, L, P = (4, 512, 128)
        D_MODEL = 128
        D_GLOBAL = 256
        HEADDIM = 32
        EPSILON = 0.001
        RMS_EPS = 1e-05

        def rmsnorm(x, g, eps=RMS_EPS):
            var = jnp.mean(jnp.square(x), axis=-1, keepdims=True)
            return x * jax.lax.rsqrt(var + eps) * g

        def _hnet_depool(h, h_patch_full, patch_lens):
            h_patch = h_patch_full[..., :D_MODEL]
            bsz, plen = (h_patch.shape[0], h_patch.shape[1])
            seqlen = h.shape[1]
            logp = jnp.full((bsz, plen), -EPSILON, dtype=jnp.float32)
            bidx = jnp.cumsum(patch_lens, axis=1) - 1
            boundary_mask = jnp.zeros((bsz, seqlen), dtype=jnp.int32)
            boundary_mask = boundary_mask.at[jnp.arange(bsz)[:, None], bidx].set(1)
            dt = (-jnp.log(-jnp.expm1(logp))).astype(h_patch.dtype)
            x = h_patch / dt[..., None]
            n_heads = D_MODEL // HEADDIM
            A = -jnp.ones((n_heads,), dtype=jnp.float32)
            bcoef = jnp.exp(logp).astype(h_patch.dtype)
            x4 = x.reshape(bsz, plen, n_heads, HEADDIM)
            a = jnp.exp(dt[:, :, None] * A[None, None, :])
            u = (dt * bcoef)[:, :, None, None] * x4
            a_b = jnp.broadcast_to(a[..., None], u.shape)

            def comb(lft, rgt):
                aL, uL = lft
                aR, uR = rgt
                return (aL * aR, uL * aR + uR)
            _, s = jax.lax.associative_scan(comb, (a_b, u), axis=1)
            depool = s.reshape(bsz, plen, D_MODEL)
            plug = jnp.clip(jnp.cumsum(boundary_mask, axis=1) - 1, 0, plen - 1)
            depool_out = depool[jnp.arange(bsz)[:, None], plug]
            return depool_out + h
        h = rmsnorm(embeds, g_res)
        h = jnp.einsum('bld,ed->ble', h, W_in) + b_in
        h_patch = rmsnorm(patch_embeds, g_init)
        return _hnet_depool(h, h_patch, patch_lens)

    def _L1_ffn_ref(x, W, b, Wg, bg):
        import jax, jax.numpy as jnp
        import numpy as np
        K = 2
        TEMP = 1.0
        gate_logits = (jnp.einsum('bsd,ed->bse', x, Wg) + bg) / TEMP
        gate_scores = jax.nn.softmax(gate_logits, axis=-1)
        topk_scores, topk_idx = jax.lax.top_k(gate_scores, K)
        expert_outputs = jnp.einsum('bsd,eod->bseo', x, W) + b
        selected = jnp.take_along_axis(expert_outputs, topk_idx[..., None], axis=2)
        output = jnp.sum(selected * topk_scores[..., None], axis=2)
        return output
    x = x + _L0_xattn_ref(ctx_2048, _layernorm(x, axis=-1), mask_BxS2_ik0, L0_xattn_b)
    x = x + _L0_ffn_ref(_layernorm(x, axis=-1), L0_ffn_k0, L0_ffn_k1, L0_ffn_k2, L0_ffn_s0, L0_ffn_s1, L0_ffn_s2)
    x = x + _L1_xattn_ref(_layernorm(x, axis=-1), ctx_2048, mask_BxS2_if0, L1_xattn_W_in, L1_xattn_b_in, L1_xattn_g_res, L1_xattn_g_init)
    x = x + _L1_ffn_ref(_layernorm(x, axis=-1), L1_ffn_W, L1_ffn_b, L1_ffn_Wg, L1_ffn_bg)
    return x

_drawn_inputs = setup_inputs


def setup_inputs(seed=0):
    import zlib

    import numpy as np

    out = dict(_drawn_inputs(seed))
    spreads = {'L1_xattn_b_in': (0.0, 0.1),
     'L1_xattn_g_res': (1.0, 0.6),
     'L1_xattn_g_init': (1.0, 0.2),
     'L1_ffn_bg': (0.0, 0.1)}
    factors = {'L1_ffn_b': 36.7}
    for name, (base, spread) in spreads.items():
        noise = np.random.default_rng([zlib.crc32(name.encode()), seed]).standard_normal(out[name].shape)
        drawn = base * np.exp(spread * noise) if base else spread * noise
        out[name] = jnp.asarray(drawn.astype(out[name].dtype))
    for name, factor in factors.items():
        out[name] = (out[name] * factor).astype(out[name].dtype)
    return out
```

```python
from contextlib import ExitStack
import math

import numpy as np

import concourse.bass as bass
from concourse import mybir

ALU = mybir.AluOpType
ACT = mybir.ActivationFunctionType
F32 = mybir.dt.float32
F16 = mybir.dt.float16
BF16 = mybir.dt.bfloat16
I32 = mybir.dt.int32
U8 = mybir.dt.uint8
U32 = mybir.dt.uint32
X = mybir.AxisListType.X

LN_EPS = 1e-5
RMS_EPS = 1e-5
NEG = -1e30
HEADS = 8
LOGP = np.float32(-0.001)
DT = -np.log(-np.expm1(LOGP))
GAIN = float(np.exp(LOGP))


class Group:

    def __init__(self, base, i):
        self.n = i * 2 + base
        self.half = i + base // 2
        self.p = base % 2
        self.static = isinstance(i, int)

    def has(self, back):
        return not self.static or self.n >= back


class Signal:

    def __init__(self, sem, per=1):
        self.sem, self.per = sem, per

    def of(self, g, k=None, back=0):
        return g.n * self.per + ((self.per if k is None else k) - back * self.per)


def build(nc, x, ctx, mask, lens, b_attn, k0, k1, k2, s0, s1, s2, w_in, b_in, g_res, g_init, w_moe, b_moe, w_gate, b_gate, out):
    B, S, D = x.shape
    NK, DC = ctx.shape[1], ctx.shape[2]
    F = k0.shape[1]
    FC = F // D
    E = w_moe.shape[0]
    G = 4
    NG = B // G
    HD = D // HEADS
    HR = 32 // HD
    R = HEADS // HR
    W = G * D
    assert S == 128 and D == 128 and W == 512 and NG % 2 == 0 and NG >= 6

    es = ExitStack()
    with es:
        def sb(name, shape, dt=F32):
            return es.enter_context(nc.sbuf_tensor(name, shape, dt))

        def signal(name, per=1):
            return Signal(es.enter_context(nc.semaphore(name)), per)

        ident = sb("ident", [128, 128])
        tri = sb("tri", [S, S], BF16)
        ones_bf = sb("ones_bf", [128, 128], BF16)
        step_i = sb("step_i", [NK, S], I32)
        step = sb("step", [NK, S])
        rank_i = sb("rank_i", [NK, 1], I32)
        rank = sb("rank", [NK, 1])
        lag_i = sb("lag_i", [NK, NK], I32)
        lag = sb("lag", [NK, NK])
        lag2 = sb("lag2", [NK, NK])
        decayT = sb("decayT", [NK, NK])
        expert_i = sb("expert_i", [128, E], I32)
        expert = sb("expert", [128, E])
        row_i = sb("row_i", [128, 2], I32)
        row_f = sb("row_f", [128, 2])
        head_scale = sb("head_scale", [128, 2])
        neg_half = sb("neg_half", [128, G])
        eps = sb("eps", [128, G, 3])
        spare_dve = sb("spare_dve", [1, 1])
        spare_pool = sb("spare_pool", [1, 3])
        lens_i = sb("lens_i", [B, NK], I32)
        lens_f = sb("lens_f", [B, NK])
        zero_b = sb("zero_b", [B, NK])
        ends = sb("ends", [B, NK])
        wrap = sb("wrap", [B, NK])
        endsT = sb("endsT", [NK, B])
        s_raw = sb("s_raw", [128, 3])
        s_sgn = sb("s_sgn", [128, 8])
        k0_u = sb("k0_u", [128, 2, F], U8)
        k1_u = sb("k1_u", [128, FC, F], U8)
        k2_u = sb("k2_u", [128, FC, D], U8)
        k0_d = sb("k0_d", [128, F])
        w1 = sb("w1", [128, F], F16)
        w2 = sb("w2", [128, FC, F], F16)
        w3 = sb("w3", [128, FC, D], F16)
        nat = sb("nat", [128, 10, 128])
        gres = sb("gres", [D, 1])
        w_inT = sb("w_inT", [D, D])
        w_moeT = sb("w_moeT", [D, E * D])
        w_gateT = sb("w_gateT", [D, E])
        bmoe = sb("bmoe", [E, D])
        bgate = sb("bgate", [128, E])
        gpatch = sb("gpatch", [NK, D])
        bin_b = sb("bin_b", [NK, D])
        battn = sb("battn", [128, 1])

        xa = sb("xa", [128, 2, W])
        cx = sb("cx", [NK, 2, G, DC])
        mask_i = sb("mask_i", [128, 2, G * NK], I32)
        mask_b = sb("mask_b", [128, G * NK], BF16)
        st = [sb(f"st{i}", [128, G, 6]) for i in range(4)]
        mv = [sb(f"mv{i}", [128, G, 2]) for i in range(4)]
        ve = [sb(f"ve{i}", [128, G]) for i in range(4)]
        rs = [sb(f"rs{i}", [128, G]) for i in range(4)]
        xn = [sb(f"xn{i}", [128, W]) for i in range(4)]
        qT = sb("qT", [128, W])
        kT = sb("kT", [128, HR, G, NK])
        vx = sb("vx", [NK, 2, G, HEADS, HD + 1])
        mx = sb("mx", [128, 2, 2, HEADS])
        pr = sb("pr", [128, 2, R, 2, HR, NK])
        prT = sb("prT", [NK, G, HEADS, S])
        rden = sb("rden", [128, G, HEADS])
        att = sb("att", [128, W])
        sq = sb("sq", [NK, G, DC])
        ss = sb("ss", [NK, G])
        ssm = sb("ssm", [NK, G])
        rk = sb("rk", [NK, G])
        hp0 = sb("hp0", [NK, G, D])
        hp = sb("hp", [NK, G, D])
        endc = sb("endc", [NK, G])
        at_end = sb("at_end", [NK, G, S], BF16)
        bm = sb("bm", [S, G], BF16)
        pick = sb("pick", [NK, 2, G, S])
        dep = sb("dep", [NK, 2, G, D])
        xb = sb("xb", [128, 2, W])
        zT = sb("zT", [128, 2, W], F16)
        h1 = sb("h1", [128, 2, FC, W], F16)
        h2 = sb("h2", [128, 2, FC, W], F16)
        xc = sb("xc", [128, 2, W])
        y3T = sb("y3T", [128, W])
        xd = sb("xd", [128, W])
        y4T = sb("y4T", [128, W])
        gl = sb("gl", [128, G, E])
        gm = sb("gm", [128, G])
        gd = sb("gd", [128, G, E])
        ge = sb("ge", [128, G, E])
        gs = sb("gs", [128, G])
        gr = sb("gr", [128, G])
        gp = sb("gp", [128, G, E])
        top = sb("top", [128, G, 8])
        topi = sb("topi", [128, G, 8], U32)
        topf = sb("topf", [128, G, 8])
        hit = sb("hit", [128, 2, G, E])
        hitw = sb("hitw", [128, 2, G, E])
        wgt = sb("wgt", [128, G, E])
        wT = sb("wT", [E, W])
        acc0 = sb("acc0", [128, W])
        acc1 = sb("acc1", [128, W])
        xo = sb("xo", [128, 2, W])

        pa = es.enter_context(nc.psum_tensor("pa", [128, 4, 512], F32))
        pb = es.enter_context(nc.psum_tensor("pb", [128, 2, 512], F32))
        pc = es.enter_context(nc.psum_tensor("pc", [128, 2, 512], F32))

        loaded = [signal(f"loaded{p}", 48) for p in range(2)]
        stored = [signal(f"stored{p}", 16) for p in range(2)]
        weights_in = signal("weights_in").sem
        made_pool = signal("made_pool").sem
        made_dve = signal("made_dve").sem
        made_pe = signal("made_pe").sem
        made_act = signal("made_act").sem
        a_bn = signal("a_bn")
        a_stats = signal("a_stats")
        a_ve = signal("a_ve")
        a_rstd = signal("a_rstd")
        a_xn = signal("a_xn")
        a_mask = signal("a_mask")
        a_endc = signal("a_endc")
        a_xT = signal("a_xT")
        a_cT = signal("a_cT")
        a_qT = signal("a_qT")
        a_kT = signal("a_kT")
        a_score = signal("a_score", 2)
        a_max = signal("a_max", 2)
        a_sub = signal("a_sub", 2)
        a_exp = signal("a_exp", 2)
        a_turn = signal("a_turn", 2)
        a_prT = signal("a_prT", 2)
        a_vx = signal("a_vx")
        a_pv = signal("a_pv")
        a_rden = signal("a_rden")
        a_att = signal("a_att")
        a_x1 = signal("a_x1")
        a_ss = signal("a_ss")
        a_ssm = signal("a_ssm")
        a_rk = signal("a_rk")
        a_hp0 = signal("a_hp0")
        a_hp = signal("a_hp")
        a_at = signal("a_at")
        a_cnt = signal("a_cnt")
        a_bm = signal("a_bm")
        a_cum = signal("a_cum")
        a_pick = signal("a_pick")
        a_scan = signal("a_scan")
        a_dep = signal("a_dep")
        b_bn = signal("b_bn")
        b_stats = signal("b_stats")
        b_ve = signal("b_ve")
        b_rstd = signal("b_rstd")
        b_xn = signal("b_xn")
        b_psum = signal("b_psum", 2 * FC + 2)
        b_hi = signal("b_hi", 2 * FC + 1)
        b_lo = signal("b_lo", 2 * FC + 1)
        b_x2 = signal("b_x2")
        c_bn = signal("c_bn", 2)
        c_stats = signal("c_stats", 2)
        c_ve = signal("c_ve", 2)
        c_rstd = signal("c_rstd", 2)
        c_xn = signal("c_xn", 2)
        c_turn = signal("c_turn", 2)
        c_yT = signal("c_yT", 2)
        c_proj = signal("c_proj")
        c_x3 = signal("c_x3")
        c_gate = signal("c_gate")
        c_gl = signal("c_gl")
        c_gm = signal("c_gm")
        c_gd = signal("c_gd")
        c_ge = signal("c_ge")
        c_gs = signal("c_gs")
        c_gr = signal("c_gr")
        c_gp = signal("c_gp")
        c_top = signal("c_top")
        c_topi = signal("c_topi")
        c_topf = signal("c_topf")
        c_hit = signal("c_hit")
        c_hitw = signal("c_hitw")
        c_wgt = signal("c_wgt")
        c_wT = signal("c_wT")
        c_wTs = signal("c_wTs")
        c_bias = signal("c_bias")
        c_acc0 = signal("c_acc0")
        c_moe = signal("c_moe", 2 * G)
        c_sum = signal("c_sum", E * G)
        c_out = signal("c_out")

        PAIRS = NG // 2 - 2

        def pipeline(eng, steps):
            steps(Group(0, 0), None, None)
            steps(Group(1, 0), Group(0, 0), None)
            steps(Group(2, 0), Group(1, 0), Group(0, 0))
            steps(Group(3, 0), Group(2, 0), Group(1, 0))
            with eng.Fori(0, PAIRS) as i:
                steps(Group(4, i), Group(3, i), Group(2, i))
                steps(Group(5, i), Group(4, i), Group(3, i))
            steps(None, Group(NG - 1, 0), Group(NG - 2, 0))
            steps(None, None, Group(NG - 1, 0))


        def bcast(ap, n):
            return ap.partition_broadcast(n)

        block = es.enter_context(nc.Block())

        @block.sync
        def _(sp):
            loads = [
                (lens_i[:], lens), (k0_u[:], k0.rearrange("(a p) f -> p a f", p=128)),
                (k1_u[:], k1.rearrange("(a p) f -> p a f", p=128)),
                (k2_u[:], k2.rearrange("(a p) f -> p a f", p=128)),
                (s_raw[:, 0:1], bcast(s0, 128)), (s_raw[:, 1:2], bcast(s1, 128)), (s_raw[:, 2:3], bcast(s2, 128)),
                (battn[:], bcast(b_attn, 128)),
                (nat[:, 0:E, :], w_moe.rearrange("e o d -> o e d")), (nat[:, E, :], w_in),
                (nat[0:E, E + 1, :], w_gate), (gres[:], g_res.rearrange("(d a) -> d a", a=1)),
                (bmoe[:], b_moe), (bgate[:], bcast(b_gate, 128)),
                (gpatch[:], bcast(g_init[0:D], NK)), (bin_b[:], bcast(b_in, NK)),
            ]
            assert len(loads) == WEIGHT_LOADS

            def load(g):
                if g.has(2):
                    sp.wait_ge(a_x1.sem, a_x1.of(g, back=2))
                    sp.wait_ge(a_vx.sem, a_vx.of(g, back=2))
                    sp.wait_ge(a_hp0.sem, a_hp0.of(g, back=2))
                    sp.wait_ge(a_mask.sem, a_mask.of(g, back=2))
                sp.dma_start(xa[:, g.p, :].rearrange("s (j d) -> s j d", j=G),
                             x[bass.ds(g.n * G, G)].rearrange("j s d -> s j d")).then_inc(loaded[g.p].sem, 16)
                sp.dma_start(cx[:, g.p], ctx[bass.ds(g.n * G, G)].rearrange("j k d -> k j d")).then_inc(loaded[g.p].sem, 16)
                sp.dma_start(mask_i[:, g.p, :],
                             mask[bass.ds(g.n * G, G)].rearrange("j k -> (j k)").partition_broadcast(128)
                             ).then_inc(loaded[g.p].sem, 16)

            def store(g):
                sp.wait_ge(c_out.sem, c_out.of(g))
                sp.dma_start(out[bass.ds(g.n * G, G)].rearrange("j s d -> s j d"),
                             xo[:, g.p, :].rearrange("s (j d) -> s j d", j=G)).then_inc(stored[g.p].sem, 16)

            load(Group(0, 0))
            for dst, src in loads:
                sp.dma_start(dst, src).then_inc(weights_in, 16)
            load(Group(1, 0))
            load(Group(2, 0))
            with sp.Fori(0, NG // 2 - 2) as i:
                load(Group(3, i))
                store(Group(0, i))
                load(Group(4, i))
                store(Group(1, i))
            load(Group(NG - 1, 0))
            for n in range(NG - 4, NG):
                store(Group(n, 0))
            for p in range(2):
                sp.wait_ge(stored[p].sem, 16 * (NG // 2))

        @block.gpsimd
        def _(pool):
            nc.gpsimd.memset(ident[:], 0.0)
            nc.gpsimd.memset(tri[:], 1.0)
            nc.gpsimd.memset(ones_bf[:], 1.0)
            nc.gpsimd.memset(neg_half[:], -0.5)
            nc.gpsimd.memset(spare_pool[:], 0.0)
            nc.gpsimd.memset(eps[:, :, 0], LN_EPS)
            nc.gpsimd.memset(eps[:, :, 1], RMS_EPS * LN_EPS / (1 + RMS_EPS))
            nc.gpsimd.memset(eps[:, :, 2], DC * RMS_EPS)
            nc.gpsimd.memset(vx[:], 1.0)
            nc.gpsimd.iota(step_i[:], [[1, S]], base=0, channel_multiplier=0)
            nc.gpsimd.iota(rank_i[:], [[0, 1]], base=1, channel_multiplier=1)
            nc.gpsimd.iota(lag_i[:], [[1, NK]], base=0, channel_multiplier=-1)
            nc.gpsimd.iota(expert_i[:], [[1, E]], base=0, channel_multiplier=0)
            nc.gpsimd.iota(row_i[:], [[0, 2]], base=0, channel_multiplier=1).then_inc(made_pool, 1)
            pool.wait_ge(made_pool, 1)
            nc.gpsimd.affine_select(out=ident[:], in_=ident[:], compare_op=ALU.not_equal, fill=1.0, base=0,
                                    pattern=[[-1, 128]], channel_multiplier=1)
            nc.gpsimd.affine_select(out=tri[:], in_=tri[:], compare_op=ALU.is_ge, fill=0.0, base=0,
                                    pattern=[[1, S]], channel_multiplier=-1)
            nc.gpsimd.tensor_copy(lag[:], lag_i[:]).then_inc(made_pool, 1)
            pool.wait_ge(made_pool, 2)
            nc.gpsimd.affine_select(out=lag2[:], in_=lag[:], compare_op=ALU.is_ge, fill=1e4, base=0,
                                    pattern=[[1, NK]], channel_multiplier=-1).then_inc(made_pool, 1)
            pool.wait_ge(weights_in, 16 * WEIGHT_LOADS)
            nc.gpsimd.tensor_scalar(gpatch[:], gpatch[:], GAIN, float(DC) ** 0.5, ALU.mult, ALU.mult).then_inc(made_pool, 1)
            pool.wait_ge(made_pool, 4)

            def rstd(n, g, stats, k, ve_sig, out_sig, k_eps=0):
                pool.wait_ge(stats.sem, stats.of(g, k))
                nc.gpsimd.tensor_tensor(ve[n][:], mv[n][:, :, 1], eps[:, :, k_eps], ALU.add).then_inc(ve_sig.sem, 1)
                pool.wait_ge(ve_sig.sem, ve_sig.of(g, k))
                nc.gpsimd.tensor_tensor(rs[n][:], ve[n][:], neg_half[:], ALU.pow).then_inc(out_sig.sem, 1)

            def patches(g):
                pool.wait_ge(loaded[g.p].sem, 48 * g.half + 48)
                if g.has(2):
                    pool.wait_ge(a_pv.sem, a_pv.of(g, back=2))
                nc.gpsimd.tensor_tensor(spare_pool[:, 0:1], spare_pool[:, 1:2], spare_pool[:, 2:3], ALU.add)
                nc.gpsimd.tensor_copy(vx[:, g.p, :, :, 0:HD],
                                      cx[:, g.p, :, D:2 * D].rearrange("k j (h d) -> k j h d", h=HEADS)
                                      ).then_inc(a_vx.sem, 1)
                pool.wait_ge(a_ss.sem, a_ss.of(g))
                nc.gpsimd.tensor_tensor(ssm[:], ss[:], eps[0:NK, :, 2], ALU.add).then_inc(a_ssm.sem, 1)
                pool.wait_ge(a_ssm.sem, a_ssm.of(g))
                nc.gpsimd.tensor_tensor(rk[:], ssm[:], neg_half[0:NK, :], ALU.pow).then_inc(a_rk.sem, 1)
                pool.wait_ge(a_rk.sem, a_rk.of(g))
                nc.gpsimd.tensor_tensor(hp0[:], cx[:, g.p, :, 0:D], rk[:].unsqueeze(2).to_broadcast([NK, G, D]),
                                        ALU.mult).then_inc(a_hp0.sem, 1)
                pool.wait_ge(a_hp0.sem, a_hp0.of(g))
                if g.has(1):
                    pool.wait_ge(a_scan.sem, a_scan.of(g, back=1))
                nc.gpsimd.tensor_tensor(hp[:], hp0[:], gpatch[:].unsqueeze(1).to_broadcast([NK, G, D]),
                                        ALU.mult).then_inc(a_hp.sem, 1)

            def boundaries(g):
                pool.wait_ge(a_endc.sem, a_endc.of(g))
                if g.has(1):
                    pool.wait_ge(a_cnt.sem, a_cnt.of(g, back=1))
                nc.gpsimd.tensor_tensor(spare_pool[:, 0:1], spare_pool[:, 1:2], spare_pool[:, 2:3], ALU.add)
                for j in range(G):
                    last = nc.gpsimd.tensor_scalar(at_end[:, j, :], step[:], endc[:, j:j + 1], None, ALU.is_equal)
                last.then_inc(a_at.sem, 1)

            def steps(a, b, c):
                if a:
                    rstd(0, a, a_stats, 1, a_ve, a_rstd)
                if b:
                    rstd(1, b, b_stats, 1, b_ve, b_rstd)
                if c:
                    rstd(2, c, c_stats, 1, c_ve, c_rstd, 1)
                if a:
                    patches(a)
                if c:
                    rstd(3, c, c_stats, 2, c_ve, c_rstd)
                if a:
                    boundaries(a)
                if c:
                    pool.wait_ge(c_sum.sem, c_sum.of(c))
                    if c.has(2):
                        pool.wait_ge(stored[c.p].sem, 16 * c.half)
                    nc.gpsimd.tensor_tensor(xo[:, c.p, :], acc0[:], acc1[:], ALU.add).then_inc(c_out.sem, 1)

            pipeline(pool, steps)

        @block.vector
        def _(dve):
            dve.wait_ge(made_pool, 3)
            nc.vector.tensor_copy(step[:], step_i[:])
            nc.vector.tensor_copy(rank[:], rank_i[:])
            nc.vector.tensor_copy(expert[:], expert_i[:])
            nc.vector.tensor_scalar(row_i[:], row_i[:], HD, None, ALU.bitwise_and)
            nc.vector.memset(zero_b[:], 0.0).then_inc(made_dve, 1)
            dve.wait_ge(made_dve, 1)
            nc.vector.tensor_copy(row_f[:], row_i[:]).then_inc(made_dve, 1)
            dve.wait_ge(made_dve, 2)
            qs = float(HD) ** -0.5
            nc.vector.tensor_scalar(head_scale[:, 0:1], row_f[:, 0:1], -qs / HD, qs, ALU.mult, ALU.add)
            nc.vector.tensor_scalar(head_scale[:, 1:2], row_f[:, 1:2], qs / HD, None, ALU.mult)
            dve.wait_ge(weights_in, 16 * WEIGHT_LOADS)
            nc.vector.tensor_copy(lens_f[:], lens_i[:])
            nc.vector.tensor_scalar(s_sgn[:, 0:3], s_raw[:], 0.0, None, ALU.is_ge)
            nc.vector.tensor_tensor(k0_d[:], k0_u[:, 0, :], k0_u[:, 1, :], ALU.subtract).then_inc(made_dve, 1)
            dve.wait_ge(made_dve, 3)
            nc.vector.tensor_tensor_scan(ends[:], lens_f[:], zero_b[:], -1.0, ALU.add, ALU.add)
            nc.vector.tensor_scalar(s_sgn[:, 3:5], s_sgn[:, 0:2], 2.0, -1.0, ALU.mult, ALU.add).then_inc(made_dve, 1)
            dve.wait_ge(made_dve, 4)
            nc.vector.tensor_scalar(wrap[:], ends[:], 0.0, float(S), ALU.is_lt, ALU.mult)
            nc.vector.tensor_tensor(s_sgn[:, 0:2], s_sgn[:, 3:5], s_raw[:, 0:2], ALU.mult)
            nc.vector.tensor_scalar(s_sgn[:, 5:6], s_sgn[:, 4:5], 0.5, None, ALU.mult)
            nc.vector.tensor_scalar(s_sgn[:, 6:7], s_sgn[:, 4:5], -0.25, None, ALU.mult)
            nc.vector.tensor_scalar(s_sgn[:, 7:8], s_sgn[:, 3:4], 2.0, None, ALU.mult).then_inc(made_dve, 1)
            dve.wait_ge(made_dve, 5)
            nc.vector.tensor_tensor(ends[:], ends[:], wrap[:], ALU.add)
            nc.vector.scalar_tensor_tensor(s_sgn[:, 2:3], s_sgn[:, 0:1], s_sgn[:, 1:2], s_raw[:, 2:3], ALU.mult, ALU.mult)
            nc.vector.tensor_scalar(w1[:], k0_d[:], s_sgn[:, 7:8], None, ALU.mult)
            nc.vector.tensor_scalar(w2[:], k1_u[:], s_sgn[:, 5:6], s_sgn[:, 6:7], ALU.mult, ALU.add)
            nc.vector.tensor_scalar(w3[:], k2_u[:], 2.0, -1.0, ALU.mult, ALU.add).then_inc(made_dve, 1)
            dve.wait_ge(made_dve, 6)
            nc.vector.tensor_scalar(s_sgn[:, 2:3], s_sgn[:, 2:3], 16.0, None, ALU.mult).then_inc(made_dve, 1)
            dve.wait_ge(made_pe, 1)
            nc.vector.tensor_copy(w_moeT[:, 0:512], pa[:, 0, :])
            nc.vector.tensor_copy(w_moeT[:, 512:1024], pa[:, 1, :])
            nc.vector.tensor_scalar(w_inT[:], pa[:, 2, 0:D], gres[:, 0:1], (1 + RMS_EPS) ** -0.5, ALU.mult, ALU.mult)
            nc.vector.tensor_copy(w_gateT[:], pa[:, 2, D:D + E])
            nc.vector.tensor_copy(endsT[:], pa[0:NK, 3, 0:B]).then_inc(made_dve, 1)
            dve.wait_ge(made_dve, 8)

            def stats(n, src, g, k, bn, sig):
                for j in range(G):
                    last = nc.vector.bn_stats(st[n][:, j, :], src[:, j * D:(j + 1) * D])
                last.then_inc(bn.sem, 1)
                dve.wait_ge(bn.sem, bn.of(g, k))
                nc.vector.memset(spare_dve[:], 0.0)
                for j in range(G):
                    last = nc.vector.bn_aggr(mv[n][:, j, :], st[n][:, j, :])
                last.then_inc(sig.sem, 1)

            def normalise(n, src, g, k, rstd, sig):
                dve.wait_ge(rstd.sem, rstd.of(g, k))
                for j in range(G):
                    last = nc.vector.tensor_scalar(xn[n][:, j * D:(j + 1) * D], src[:, j * D:(j + 1) * D],
                                                   mv[n][:, j, 0:1], rs[n][:, j:j + 1], ALU.subtract, ALU.mult)
                last.then_inc(sig.sem, 1)

            def a_start(g):
                dve.wait_ge(loaded[g.p].sem, 48 * g.half + 48)
                stats(0, xa[:, g.p, :], g, 1, a_bn, a_stats)
                if g.has(1):
                    dve.wait_ge(a_score.sem, a_score.of(g, back=1))
                nc.vector.tensor_scalar(mask_b[:], mask_i[:, g.p, :], -1.0, -NEG, ALU.add, ALU.mult).then_inc(a_mask.sem, 1)
                if g.has(1):
                    dve.wait_ge(a_at.sem, a_at.of(g, back=1))
                nc.vector.tensor_copy(endc[:], endsT[:, bass.ds(g.n * G, G)]).then_inc(a_endc.sem, 1)

            def a_normalise(g):
                if g.has(1):
                    dve.wait_ge(a_xT.sem, a_xT.of(g, back=1))
                normalise(0, xa[:, g.p, :], g, 1, a_rstd, a_xn)

            def a_softmax(g, q):
                scores = pa[:, :, 0:2 * HR * NK].rearrange("p r (j e k) -> p r j e k", j=2, e=HR)
                dve.wait_ge(a_score.sem, a_score.of(g, q + 1))
                for j in range(2):
                    last = nc.vector.tensor_reduce(mx[:, q, j, :].rearrange("p (r e) -> p r e", r=R), scores[:, :, j], X, ALU.max)
                last.then_inc(a_max.sem, 1)
                dve.wait_ge(a_max.sem, a_max.of(g, q + 1))
                if g.has(1):
                    dve.wait_ge(a_turn.sem, a_turn.of(g, q + 1, back=1))
                for j in range(2):
                    last = nc.vector.tensor_tensor(
                        pr[:, q, :, j], scores[:, :, j],
                        mx[:, q, j, :].rearrange("p (r e) -> p r e", r=R).unsqueeze(3).to_broadcast([128, R, HR, NK]),
                        ALU.subtract)
                last.then_inc(a_sub.sem, 1)

            def a_boundary(g):
                dve.wait_ge(a_cnt.sem, a_cnt.of(g))
                nc.vector.tensor_scalar(bm[:], pa[:, 3, 0:G], 1.0, None, ALU.min).then_inc(a_bm.sem, 1)

            def a_depool(g):
                dve.wait_ge(a_scan.sem, a_scan.of(g))
                if g.has(2):
                    dve.wait_ge(c_proj.sem, c_proj.of(g, back=2))
                nc.vector.tensor_tensor(dep[:, g.p], pa[0:NK, 2, :].rearrange("k (j d) -> k j d", j=G),
                                        bin_b[:].unsqueeze(1).to_broadcast([NK, G, D]), ALU.add).then_inc(a_dep.sem, 1)
                dve.wait_ge(a_cum.sem, a_cum.of(g))
                nc.vector.tensor_scalar(pick[:, g.p], pa[0:NK, 3, :].rearrange("k (j s) -> k j s", j=G), 1.0, rank[:, 0:1],
                                        ALU.max, ALU.is_equal).then_inc(a_pick.sem, 1)

            def a_end(g):
                dve.wait_ge(a_pv.sem, a_pv.of(g))
                po = pa[:, 0:2, 0:2 * HEADS * (HD + 1)].rearrange("p b (j h c) -> p b j h c", j=2, h=HEADS)
                for b in range(2):
                    last = nc.vector.reciprocal(rden[:, 2 * b:2 * b + 2, :], po[:, b, :, :, HD])
                last.then_inc(a_rden.sem, 1)
                dve.wait_ge(a_rden.sem, a_rden.of(g))
                for j in range(G):
                    last = nc.vector.tensor_tensor(
                        att[:, j * D:(j + 1) * D].rearrange("p (h c) -> p h c", h=HEADS), po[:, j // 2, j % 2, :, 0:HD],
                        rden[:, j, :].unsqueeze(2).to_broadcast([128, HEADS, HD]), ALU.mult)
                last.then_inc(a_att.sem, 1)
                dve.wait_ge(a_att.sem, a_att.of(g))
                nc.vector.tensor_tensor(xb[:, g.p, :], att[:], xa[:, g.p, :], ALU.add).then_inc(a_x1.sem, 1)

            def b_start(g):
                dve.wait_ge(a_x1.sem, a_x1.of(g))
                stats(1, xb[:, g.p, :], g, 1, b_bn, b_stats)

            def b_normalise(g):
                if g.has(1):
                    dve.wait_ge(b_psum.sem, b_psum.of(g, 1, back=1))
                normalise(1, xb[:, g.p, :], g, 1, b_rstd, b_xn)

            def b_low(g, k):
                dve.wait_ge(b_hi.sem, b_hi.of(g, k + 1))
                src = pb[:, k % 2, :]
                if k == 0:
                    last = nc.vector.tensor_tensor(zT[:, 1, :], src, zT[:, 0, :], ALU.subtract)
                else:
                    h = h1 if k <= FC else h2
                    last = nc.vector.scalar_tensor_tensor(h[:, 1, (k - 1) % FC, :], src, 0.0, h[:, 0, (k - 1) % FC, :],
                                                          ALU.max, ALU.subtract)
                last.then_inc(b_lo.sem, 1)

            def b_end(g):
                k = 2 * FC + 1
                dve.wait_ge(b_psum.sem, b_psum.of(g, k + 1))
                nc.vector.scalar_tensor_tensor(xc[:, g.p, :], pb[:, k % 2, :], s_sgn[:, 2:3], xb[:, g.p, :],
                                               ALU.mult, ALU.add).then_inc(b_x2.sem, 1)

            def c_start(g):
                dve.wait_ge(b_x2.sem, b_x2.of(g))
                stats(2, xc[:, g.p, :], g, 1, c_bn, c_stats)

            def c_normalise(g, k):
                if g.has(1):
                    dve.wait_ge(c_turn.sem, c_turn.of(g, k, back=1))
                normalise(1 + k, xc[:, g.p, :] if k == 1 else xd[:], g, k, c_rstd, c_xn)

            def c_mid(g):
                dve.wait_ge(c_proj.sem, c_proj.of(g))
                nc.vector.tensor_tensor(xd[:], pc[:, 1, :], xc[:, g.p, :], ALU.add).then_inc(c_x3.sem, 1)
                dve.wait_ge(c_x3.sem, c_x3.of(g))
                stats(3, xd[:], g, 2, c_bn, c_stats)

            def c_gates(g):
                dve.wait_ge(c_gate.sem, c_gate.of(g))
                nc.vector.tensor_tensor(gl[:], pc[:, 1, 0:G * E].rearrange("p (j e) -> p j e", j=G),
                                        bgate[:].unsqueeze(1).to_broadcast([128, G, E]), ALU.add).then_inc(c_gl.sem, 1)
                dve.wait_ge(c_gl.sem, c_gl.of(g))
                nc.vector.tensor_reduce(gm[:], gl[:], X, ALU.max).then_inc(c_gm.sem, 1)
                dve.wait_ge(c_gm.sem, c_gm.of(g))
                nc.vector.tensor_tensor(gd[:], gl[:], gm[:].unsqueeze(2).to_broadcast([128, G, E]),
                                        ALU.subtract).then_inc(c_gd.sem, 1)

            def c_gates2(g):
                dve.wait_ge(c_ge.sem, c_ge.of(g))
                nc.vector.tensor_reduce(gs[:], ge[:], X, ALU.add).then_inc(c_gs.sem, 1)
                dve.wait_ge(c_gs.sem, c_gs.of(g))
                nc.vector.reciprocal(gr[:], gs[:]).then_inc(c_gr.sem, 1)
                dve.wait_ge(c_gr.sem, c_gr.of(g))
                nc.vector.tensor_tensor(gp[:], ge[:], gr[:].unsqueeze(2).to_broadcast([128, G, E]),
                                        ALU.mult).then_inc(c_gp.sem, 1)
                dve.wait_ge(c_gp.sem, c_gp.of(g))
                nc.vector.memset(spare_dve[:], 0.0)
                for j in range(G):
                    last = nc.vector.max(top[:, j, :], gp[:, j, :])
                last.then_inc(c_top.sem, 1)
                dve.wait_ge(c_top.sem, c_top.of(g))
                nc.vector.memset(spare_dve[:], 0.0)
                for j in range(G):
                    last = nc.vector.max_index(topi[:, j, :], top[:, j, :], gp[:, j, :])
                last.then_inc(c_topi.sem, 1)
                dve.wait_ge(c_topi.sem, c_topi.of(g))
                nc.vector.tensor_copy(topf[:], topi[:]).then_inc(c_topf.sem, 1)
                dve.wait_ge(c_topf.sem, c_topf.of(g))
                for t in range(2):
                    last = nc.vector.tensor_tensor(hit[:, t], expert[:].unsqueeze(1).to_broadcast([128, G, E]),
                                                   topf[:, :, t:t + 1].to_broadcast([128, G, E]), ALU.is_equal)
                last.then_inc(c_hit.sem, 1)
                dve.wait_ge(c_hit.sem, c_hit.of(g))
                for t in range(2):
                    last = nc.vector.tensor_tensor(hitw[:, t], hit[:, t], top[:, :, t:t + 1].to_broadcast([128, G, E]), ALU.mult)
                last.then_inc(c_hitw.sem, 1)
                dve.wait_ge(c_hitw.sem, c_hitw.of(g))
                nc.vector.tensor_tensor(wgt[:], hitw[:, 0], hitw[:, 1], ALU.add).then_inc(c_wgt.sem, 1)

            def c_bias_in(g):
                if g.has(1):
                    dve.wait_ge(c_out.sem, c_out.of(g, back=1))
                dve.wait_ge(c_bias.sem, c_bias.of(g))
                nc.vector.tensor_tensor(acc0[:], pc[:, 1, :], xd[:], ALU.add).then_inc(c_acc0.sem, 1)
                dve.wait_ge(c_acc0.sem, c_acc0.of(g))

            def c_experts(g, j, half):
                dve.wait_ge(c_moe.sem, c_moe.of(g, 2 * j + half + 1))
                cols = slice(j * D, (j + 1) * D)
                for e in range(4 * half, 4 * half + 4):
                    src = pc[:, half, (e % 4) * D:(e % 4 + 1) * D]
                    w = wgt[:, j, e:e + 1]
                    acc = acc1 if e % 2 else acc0
                    if e >= 2:
                        dve.wait_ge(c_sum.sem, c_sum.of(g, E * j + e - 1))
                    if e == 1:
                        last = nc.vector.tensor_scalar(acc[:, cols], src, w, None, ALU.mult)
                    else:
                        last = nc.vector.scalar_tensor_tensor(acc[:, cols], src, w, acc[:, cols], ALU.mult, ALU.add)
                    last.then_inc(c_sum.sem, 1)

            def steps(a, b, c):
                if a:
                    a_start(a)
                if b:
                    b_start(b)
                if c:
                    c_start(c)
                if a:
                    a_normalise(a)
                if b:
                    b_normalise(b)
                if c:
                    c_normalise(c, 1)
                if b:
                    b_low(b, 0)
                if a:
                    a_softmax(a, 0)
                if b:
                    b_low(b, 1)
                if c:
                    c_mid(c)
                if b:
                    b_low(b, 2)
                if a:
                    a_softmax(a, 1)
                if c:
                    c_normalise(c, 2)
                if b:
                    b_low(b, 3)
                    b_low(b, 4)
                if c:
                    c_gates(c)
                if b:
                    b_low(b, 5)
                if c:
                    c_gates2(c)
                if b:
                    b_low(b, 6)
                if c:
                    c_bias_in(c)
                    c_experts(c, 0, 0)
                if b:
                    b_low(b, 7)
                if c:
                    c_experts(c, 0, 1)
                    c_experts(c, 1, 0)
                if a:
                    a_boundary(a)
                if b:
                    b_low(b, 8)
                if c:
                    c_experts(c, 1, 1)
                    c_experts(c, 2, 0)
                if a:
                    a_depool(a)
                if c:
                    c_experts(c, 2, 1)
                    c_experts(c, 3, 0)
                if b:
                    b_end(b)
                if c:
                    c_experts(c, 3, 1)
                if a:
                    a_end(a)

            pipeline(dve, steps)

        @block.scalar
        def _(act):
            act.wait_ge(made_pool, 3)
            nc.scalar.activation(decayT[:], lag2[:], ACT.Exp, scale=-float(DT)).then_inc(made_act, 1)
            act.wait_ge(made_dve, 8)

            def a_turned(g):
                act.wait_ge(a_xT.sem, a_xT.of(g))
                if g.has(1):
                    act.wait_ge(a_score.sem, a_score.of(g, back=1))
                nc.scalar.activation(qT[:], pa[:, 0, :], ACT.Copy).then_inc(a_qT.sem, 1)
                act.wait_ge(a_cT.sem, a_cT.of(g))
                for e in range(HR):
                    last = nc.scalar.activation(kT[:, e], pa[:, 1, 0:G * NK].rearrange("p (j k) -> p j k", j=G),
                                                ACT.Copy, scale=head_scale[:, e:e + 1])
                last.then_inc(a_kT.sem, 1)

            def a_squares(g):
                act.wait_ge(loaded[g.p].sem, 48 * g.half + 48)
                if g.has(1):
                    act.wait_ge(a_ssm.sem, a_ssm.of(g, back=1))
                for j in range(G):
                    last = nc.scalar.activation(sq[:, j, :], cx[:, g.p, j, :], ACT.Square, accum_out=ss[:, j:j + 1])
                last.then_inc(a_ss.sem, 1)

            def a_exponent(g, q):
                act.wait_ge(a_sub.sem, a_sub.of(g, q + 1))
                flat = pr[:, q].rearrange("p r j e k -> p (r j e k)")
                nc.scalar.activation(flat, flat, ACT.Exp).then_inc(a_exp.sem, 1)

            def a_turned_back(g, q):
                act.wait_ge(a_turn.sem, a_turn.of(g, q + 1))
                if g.has(1):
                    act.wait_ge(a_pv.sem, a_pv.of(g, back=1))
                for j in range(2):
                    last = nc.scalar.activation(prT[:, 2 * q + j].rearrange("k (b h) s -> k b (h s)", b=2),
                                                pa[0:NK, 2 * j:2 * j + 2, :], ACT.Copy)
                last.then_inc(a_prT.sem, 1)

            def b_high(g, k):
                act.wait_ge(b_psum.sem, b_psum.of(g, k + 1))
                src = pb[:, k % 2, :]
                if k == 0:
                    if g.has(1):
                        act.wait_ge(b_psum.sem, b_psum.of(g, 1 + FC, back=1))
                    last = nc.scalar.activation(zT[:, 0, :], src, ACT.Copy)
                else:
                    h = h1 if k <= FC else h2
                    last = nc.scalar.activation(h[:, 0, (k - 1) % FC, :], src, ACT.Relu)
                last.then_inc(b_hi.sem, 1)

            def c_turned(g, k):
                act.wait_ge(c_turn.sem, c_turn.of(g, k))
                if k == 1:
                    if g.has(1):
                        act.wait_ge(c_proj.sem, c_proj.of(g, back=1))
                    nc.scalar.activation(y3T[:], pc[:, 0, :], ACT.Copy).then_inc(c_yT.sem, 1)
                else:
                    if g.has(1):
                        act.wait_ge(c_moe.sem, c_moe.of(g, back=1))
                    nc.scalar.activation(y4T[:], pc[:, 0, :], ACT.Copy).then_inc(c_yT.sem, 1)

            def c_gate_exp(g):
                act.wait_ge(c_gd.sem, c_gd.of(g))
                nc.scalar.activation(ge[:], gd[:], ACT.Exp).then_inc(c_ge.sem, 1)

            def c_weights_turned(g):
                act.wait_ge(c_wT.sem, c_wT.of(g))
                nc.scalar.activation(wT[:], pc[0:E, 0, :], ACT.Copy).then_inc(c_wTs.sem, 1)

            def steps(a, b, c):
                if a:
                    a_squares(a)
                    a_turned(a)
                if b:
                    b_high(b, 0)
                if c:
                    c_turned(c, 1)
                if b:
                    b_high(b, 1)
                if a:
                    a_exponent(a, 0)
                if b:
                    b_high(b, 2)
                    b_high(b, 3)
                if c:
                    c_turned(c, 2)
                if a:
                    a_exponent(a, 1)
                if b:
                    b_high(b, 4)
                if a:
                    a_turned_back(a, 0)
                if c:
                    c_gate_exp(c)
                if b:
                    b_high(b, 5)
                    b_high(b, 6)
                if a:
                    a_turned_back(a, 1)
                if c:
                    c_weights_turned(c)
                if b:
                    b_high(b, 7)
                    b_high(b, 8)

            pipeline(act, steps)

        @block.tensor
        def _(pe):
            pe.wait_ge(made_pool, 2 + 1)
            pe.wait_ge(weights_in, 16 * WEIGHT_LOADS)
            for e in range(E):
                pe.transpose(pa[:, e // 4, (e % 4) * D:(e % 4 + 1) * D], nat[:, e, :], ident[:])
            pe.transpose(pa[:, 2, 0:D], nat[:, E, :], ident[:])
            pe.transpose(pa[:, 2, D:D + E], nat[0:E, E + 1, :], ident[0:E, 0:E])
            pe.wait_ge(made_dve, 6)
            pe.transpose(pa[0:NK, 3, 0:B], ends[:], ident[0:B, 0:B]).then_inc(made_pe, 1)
            pe.wait_ge(made_dve, 8)
            pe.wait_ge(made_act, 1)
            pe.wait_ge(made_pool, 4)

            def turn4(dst, src, rows=128):
                for j in range(G):
                    last = pe.transpose(dst[:, j * rows:(j + 1) * rows], src(j), ident[0:rows, 0:rows])
                return last

            def a_turns(g):
                if g.has(1):
                    pe.wait_ge(a_x1.sem, a_x1.of(g, back=1))
                    pe.wait_ge(a_att.sem, a_att.of(g, back=1))
                pe.wait_ge(loaded[g.p].sem, 48 * g.half + 48)
                turn4(pa[:, 1, :], lambda j: cx[:, g.p, j, 0:D], NK).then_inc(a_cT.sem, 1)
                pe.wait_ge(a_xn.sem, a_xn.of(g))
                turn4(pa[:, 0, :], lambda j: xn[0][:, j * D:(j + 1) * D]).then_inc(a_xT.sem, 1)

            def a_scores(g, q):
                if q == 0:
                    pe.wait_ge(a_qT.sem, a_qT.of(g))
                    pe.wait_ge(a_kT.sem, a_kT.of(g))
                    pe.wait_ge(a_mask.sem, a_mask.of(g))
                    if g.has(1):
                        pe.wait_ge(a_dep.sem, a_dep.of(g, back=1))
                        pe.wait_ge(a_pick.sem, a_pick.of(g, back=1))
                else:
                    pe.wait_ge(a_sub.sem, a_sub.of(g, q))
                n = HR * NK
                for r in range(R):
                    rows = slice(32 * r, 32 * r + 32)
                    row = slice(32 * r, 32 * r + 1)
                    pe.matmul(pa[:, r, 0:2 * n], ones_bf[row, :],
                              mask_b[row, 2 * q * NK:(2 * q + 2) * NK].rearrange("o (j k) -> o j k", j=2)
                              .unsqueeze(2).to_broadcast([1, 2, HR, NK]), start=True, stop=False)
                for j in range(2):
                    for r in range(R):
                        rows = slice(32 * r, 32 * r + 32)
                        b = 2 * q + j
                        last = pe.matmul(pa[:, r, j * n:(j + 1) * n], qT[rows, b * S:(b + 1) * S], kT[rows, :, b, :],
                                         start=False, stop=(j == 1))
                last.then_inc(a_score.sem, 1)

            def a_turn_back(g, q):
                if q == 0:
                    pe.wait_ge(a_sub.sem, a_sub.of(g, 2))
                else:
                    pe.wait_ge(a_prT.sem, a_prT.of(g, 1))
                pe.wait_ge(a_exp.sem, a_exp.of(g, q + 1))
                for j in range(2):
                    for h in range(HEADS):
                        last = pe.transpose(pa[0:NK, 2 * j + h // 4, (h % 4) * S:(h % 4 + 1) * S],
                                            pr[:, q, h // HR, j, h % HR, :], ident[:])
                last.then_inc(a_turn.sem, 1)

            def a_values(g, j):
                if j == 0:
                    pe.wait_ge(a_prT.sem, a_prT.of(g, 2))
                    pe.wait_ge(a_vx.sem, a_vx.of(g))
                for h in range(HEADS):
                    at = ((j % 2) * HEADS + h) * (HD + 1)
                    last = pe.matmul(pa[:, j // 2, at:at + HD + 1], prT[:, j, h, :], vx[:, g.p, j, h, :],
                                     start=True, stop=True)
                if j == G - 1:
                    last.then_inc(a_pv.sem, 1)

            def a_count(g):
                pe.wait_ge(a_prT.sem, a_prT.of(g, 2))
                pe.wait_ge(a_at.sem, a_at.of(g))
                for j in range(G):
                    last = pe.matmul(pa[:, 3, j:j + 1], at_end[:, j, :], ones_bf[0:NK, 0:1], start=True, stop=True)
                last.then_inc(a_cnt.sem, 1)
                pe.wait_ge(a_hp.sem, a_hp.of(g))
                pe.matmul(pa[0:NK, 2, :], decayT[:], hp[:].rearrange("k j d -> k (j d)"), start=True, stop=True
                          ).then_inc(a_scan.sem, 1)

            def a_cumulate(g):
                pe.wait_ge(a_bm.sem, a_bm.of(g))
                for j in range(G):
                    last = pe.matmul(pa[0:NK, 3, j * S:(j + 1) * S], bm[:, j:j + 1].to_broadcast([S, NK]), tri[:],
                                     start=True, stop=True)
                last.then_inc(a_cum.sem, 1)

            def b_turns(g):
                pe.wait_ge(b_xn.sem, b_xn.of(g))
                if g.has(1):
                    pe.wait_ge(b_lo.sem, b_lo.of(g, back=1))
                turn4(pb[:, 0, :], lambda j: xn[1][:, j * D:(j + 1) * D]).then_inc(b_psum.sem, 1)

            def b_layer(g, k):
                c = (k - 1) % FC
                if k >= 2:
                    pe.wait_ge(b_lo.sem, b_lo.of(g, k - 1))
                elif g.has(1):
                    pe.wait_ge(b_x2.sem, b_x2.of(g, back=1))
                if k <= FC:
                    pe.wait_ge(b_lo.sem, b_lo.of(g, 1))
                    for part in range(2):
                        last = pe.matmul(pb[:, k % 2, :], w1[:, c * 128:(c + 1) * 128], zT[:, part, :],
                                         start=(part == 0), stop=(part == 1))
                else:
                    for i in range(FC):
                        if k == FC + 1:
                            pe.wait_ge(b_lo.sem, b_lo.of(g, 2 + i))
                        for part in range(2):
                            last = pe.matmul(pb[:, k % 2, :], w2[:, i, c * 128:(c + 1) * 128], h1[:, part, i, :],
                                             start=(i == 0 and part == 0), stop=(i == FC - 1 and part == 1))
                last.then_inc(b_psum.sem, 1)

            def b_last(g):
                k = 2 * FC + 1
                pe.wait_ge(b_lo.sem, b_lo.of(g))
                for j in range(G):
                    for i in range(FC):
                        for part in range(2):
                            last = pe.matmul(pb[:, k % 2, j * D:(j + 1) * D], h2[:, part, i, j * S:(j + 1) * S], w3[:, i, :],
                                             start=(i == 0 and part == 0), stop=(i == FC - 1 and part == 1))
                last.then_inc(b_psum.sem, 1)

            def c_turns(g, k):
                pe.wait_ge(c_xn.sem, c_xn.of(g, k))
                if k == 1 and g.has(1):
                    pe.wait_ge(c_sum.sem, c_sum.of(g, back=1))
                turn4(pc[:, 0, :], lambda j: xn[1 + k][:, j * D:(j + 1) * D]).then_inc(c_turn.sem, 1)

            def c_project(g):
                pe.wait_ge(c_yT.sem, c_yT.of(g, 1))
                pe.wait_ge(a_dep.sem, a_dep.of(g))
                pe.wait_ge(a_pick.sem, a_pick.of(g))
                for j in range(G):
                    cols = slice(j * S, (j + 1) * S)
                    pe.matmul(pc[:, 1, cols], y3T[:, cols], w_inT[:], start=True, stop=False)
                    last = pe.matmul(pc[:, 1, cols], pick[:, g.p, j, :], dep[:, g.p, j, :], start=False, stop=True)
                last.then_inc(c_proj.sem, 1)

            def c_gate_scores(g):
                pe.wait_ge(c_yT.sem, c_yT.of(g, 2))
                for j in range(G):
                    last = pe.matmul(pc[:, 1, j * E:(j + 1) * E], y4T[:, j * S:(j + 1) * S], w_gateT[:], start=True, stop=True)
                last.then_inc(c_gate.sem, 1)

            def c_weight_turns(g):
                pe.wait_ge(c_wgt.sem, c_wgt.of(g))
                for j in range(G):
                    last = pe.transpose(pc[0:E, 0, j * S:(j + 1) * S], wgt[:, j, :], ident[:])
                last.then_inc(c_wT.sem, 1)

            def c_biases(g):
                pe.wait_ge(c_wTs.sem, c_wTs.of(g))
                for j in range(G):
                    last = pe.matmul(pc[:, 1, j * D:(j + 1) * D], wT[:, j * S:(j + 1) * S], bmoe[:], start=True, stop=True)
                last.then_inc(c_bias.sem, 1)

            def c_experts(g, j, half):
                if j == 0 and half == 1:
                    pe.wait_ge(c_acc0.sem, c_acc0.of(g))
                if j > 0:
                    pe.wait_ge(c_sum.sem, c_sum.of(g, E * (j - 1) + 4 * (half + 1)))
                pe.matmul(pc[:, half, :], y4T[:, j * S:(j + 1) * S], w_moeT[:, half * 512:(half + 1) * 512],
                          start=True, stop=True).then_inc(c_moe.sem, 1)

            def steps(a, b, c):
                if a:
                    a_turns(a)
                if b:
                    b_turns(b)
                if c:
                    c_turns(c, 1)
                if b:
                    b_layer(b, 1)
                if a:
                    a_scores(a, 0)
                if c:
                    c_project(c)
                if b:
                    b_layer(b, 2)
                    b_layer(b, 3)
                if a:
                    a_scores(a, 1)
                if c:
                    c_turns(c, 2)
                if b:
                    b_layer(b, 4)
                if c:
                    c_gate_scores(c)
                if a:
                    a_turn_back(a, 0)
                if b:
                    b_layer(b, 5)
                if c:
                    c_weight_turns(c)
                if a:
                    a_turn_back(a, 1)
                if b:
                    b_layer(b, 6)
                if c:
                    c_biases(c)
                    c_experts(c, 0, 0)
                    c_experts(c, 0, 1)
                if b:
                    b_layer(b, 7)
                if a:
                    a_count(a)
                if c:
                    c_experts(c, 1, 0)
                if a:
                    a_values(a, 0)
                if c:
                    c_experts(c, 1, 1)
                if b:
                    b_layer(b, 8)
                if a:
                    a_cumulate(a)
                    a_values(a, 1)
                if c:
                    c_experts(c, 2, 0)
                if a:
                    a_values(a, 2)
                if c:
                    c_experts(c, 2, 1)
                    c_experts(c, 3, 0)
                if b:
                    b_last(b)
                if c:
                    c_experts(c, 3, 1)
                if a:
                    a_values(a, 3)

            pipeline(pe, steps)


WEIGHT_LOADS = 16

_INS = ['x', 'ctx_2048', 'mask_BxS2_ik0', 'mask_BxS2_if0', 'L0_xattn_b', 'L0_ffn_k0', 'L0_ffn_k1', 'L0_ffn_k2',
        'L0_ffn_s0', 'L0_ffn_s1', 'L0_ffn_s2', 'L1_xattn_W_in', 'L1_xattn_b_in', 'L1_xattn_g_res', 'L1_xattn_g_init',
        'L1_ffn_W', 'L1_ffn_b', 'L1_ffn_Wg', 'L1_ffn_bg']


def kernel(**inputs):
    from concourse import bacc
    from concourse.bass_utils import run_bass_kernel_spmd

    nc = bacc.Bacc("TRN2", target_bir_lowering=False, num_devices=1)
    arrays, args = {}, []
    for name in _INS:
        a = np.ascontiguousarray(inputs[name])
        if a.ndim == 0:
            a = a.reshape(1)
        arrays[f"in_{name}"] = a
        args.append(nc.dram_tensor(f"in_{name}", a.shape, mybir.dt.from_np(a.dtype), kind="ExternalInput").ap())
    out = nc.dram_tensor("out_x", inputs['x'].shape, F32, kind="ExternalOutput").ap()
    build(nc, *args, out)
    r = run_bass_kernel_spmd(nc, [arrays], core_ids=[0])
    return r.results[0]["out_x"]
```

```python
from contextlib import ExitStack
import math

import numpy as np

import concourse.bass as bass
from concourse import mybir

ALU = mybir.AluOpType
ACT = mybir.ActivationFunctionType
F32 = mybir.dt.float32
F16 = mybir.dt.float16
BF16 = mybir.dt.bfloat16
I32 = mybir.dt.int32
U8 = mybir.dt.uint8
U32 = mybir.dt.uint32
X = mybir.AxisListType.X

LN_EPS = 1e-5
RMS_EPS = 1e-5
NEG = -1e30
HEADS = 8
LOGP = np.float32(-0.001)
DT = -np.log(-np.expm1(LOGP))
GAIN = float(np.exp(LOGP))


class Group:

    def __init__(self, base, i):
        self.n = i * 2 + base
        self.half = i + base // 2
        self.p = base % 2
        self.static = isinstance(i, int)

    def has(self, back):
        return not self.static or self.n >= back


class Signal:

    def __init__(self, sem, per=1):
        self.sem, self.per = sem, per

    def of(self, g, k=None, back=0):
        return g.n * self.per + ((self.per if k is None else k) - back * self.per)


def build(nc, x, ctx, mask, lens, b_attn, k0, k1, k2, s0, s1, s2, w_in, b_in, g_res, g_init, w_moe, b_moe, w_gate, b_gate, out):
    B, S, D = x.shape
    NK, DC = ctx.shape[1], ctx.shape[2]
    F = k0.shape[1]
    FC = F // D
    E = w_moe.shape[0]
    G = 4
    NG = B // G
    HD = D // HEADS
    HR = 32 // HD
    R = HEADS // HR
    W = G * D
    assert S == 128 and D == 128 and W == 512 and NG % 2 == 0 and NG >= 6

    es = ExitStack()
    with es:
        def sb(name, shape, dt=F32):
            return es.enter_context(nc.sbuf_tensor(name, shape, dt))

        def signal(name, per=1):
            return Signal(es.enter_context(nc.semaphore(name)), per)

        ident = sb("ident", [128, 128])
        tri = sb("tri", [S, S], BF16)
        ones_bf = sb("ones_bf", [128, 128], BF16)
        step_i = sb("step_i", [NK, S], I32)
        step = sb("step", [NK, S])
        rank_i = sb("rank_i", [NK, 1], I32)
        rank = sb("rank", [NK, 1])
        lag_i = sb("lag_i", [NK, NK], I32)
        lag = sb("lag", [NK, NK])
        lag2 = sb("lag2", [NK, NK])
        decayT = sb("decayT", [NK, NK])
        expert_i = sb("expert_i", [128, E], I32)
        expert = sb("expert", [128, E])
        row_i = sb("row_i", [128, 2], I32)
        row_f = sb("row_f", [128, 2])
        head_scale = sb("head_scale", [128, 2])
        neg_half = sb("neg_half", [128, G])
        eps = sb("eps", [128, G, 3])
        spare_dve = sb("spare_dve", [1, 1])
        spare_pool = sb("spare_pool", [1, 3])
        lens_i = sb("lens_i", [B, NK], I32)
        lens_f = sb("lens_f", [B, NK])
        zero_b = sb("zero_b", [B, NK])
        ends = sb("ends", [B, NK])
        wrap = sb("wrap", [B, NK])
        endsT = sb("endsT", [NK, B])
        s_raw = sb("s_raw", [128, 3])
        s_sgn = sb("s_sgn", [128, 8])
        k0_u = sb("k0_u", [128, 2, F], U8)
        k1_u = sb("k1_u", [128, FC, F], U8)
        k2_u = sb("k2_u", [128, FC, D], U8)
        k0_d = sb("k0_d", [128, F])
        w1 = sb("w1", [128, F], F16)
        w2 = sb("w2", [128, FC, F], F16)
        w3 = sb("w3", [128, FC, D], F16)
        nat = sb("nat", [128, 10, 128])
        gres = sb("gres", [D, 1])
        w_inT = sb("w_inT", [D, D])
        w_moeT = sb("w_moeT", [D, E * D])
        w_gateT = sb("w_gateT", [D, E])
        bmoe = sb("bmoe", [E, D])
        bgate = sb("bgate", [128, E])
        gpatch = sb("gpatch", [NK, D])
        bin_b = sb("bin_b", [NK, D])
        battn = sb("battn", [128, 1])

        xa = sb("xa", [128, 2, W])
        cx = sb("cx", [NK, 2, G, DC])
        mask_i = sb("mask_i", [128, 2, G * NK], I32)
        mask_b = sb("mask_b", [128, G * NK], BF16)
        st = [sb(f"st{i}", [128, G, 6]) for i in range(4)]
        mv = [sb(f"mv{i}", [128, G, 2]) for i in range(4)]
        ve = [sb(f"ve{i}", [128, G]) for i in range(4)]
        rs = [sb(f"rs{i}", [128, G]) for i in range(4)]
        xn = [sb(f"xn{i}", [128, W]) for i in range(4)]
        qT = sb("qT", [128, W])
        kT = sb("kT", [128, HR, G, NK])
        vx = sb("vx", [NK, 2, G, HEADS, HD + 1])
        mx = sb("mx", [128, 2, 2, HEADS])
        pr = sb("pr", [128, 2, R, 2, HR, NK])
        prT = sb("prT", [NK, G, HEADS, S])
        rden = sb("rden", [128, G, HEADS])
        att = sb("att", [128, W])
        sq = sb("sq", [NK, G, DC])
        ss = sb("ss", [NK, G])
        ssm = sb("ssm", [NK, G])
        rk = sb("rk", [NK, G])
        hp0 = sb("hp0", [NK, G, D])
        hp = sb("hp", [NK, G, D])
        endc = sb("endc", [NK, G])
        at_end = sb("at_end", [NK, G, S], BF16)
        bm = sb("bm", [S, G], BF16)
        pick = sb("pick", [NK, 2, G, S])
        dep = sb("dep", [NK, 2, G, D])
        xb = sb("xb", [128, 2, W])
        zT = sb("zT", [128, 2, W], F16)
        h1 = sb("h1", [128, 2, FC, W], F16)
        h2 = sb("h2", [128, 2, FC, W], F16)
        xc = sb("xc", [128, 2, W])
        y3T = sb("y3T", [128, W])
        xd = sb("xd", [128, W])
        y4T = sb("y4T", [128, 2, W])
        gl = sb("gl", [128, G, E])
        gm = sb("gm", [128, G])
        gd = sb("gd", [128, G, E])
        ge = sb("ge", [128, G, E])
        gs = sb("gs", [128, G])
        gr = sb("gr", [128, G])
        gp = sb("gp", [128, G, E])
        top = sb("top", [128, G, 8])
        topi = sb("topi", [128, G, 8], U32)
        topf = sb("topf", [128, G, 8])
        hit = sb("hit", [128, 2, G, E])
        hitw = sb("hitw", [128, 2, G, E])
        wgt = sb("wgt", [128, 2, G, E])
        wT = sb("wT", [E, W])
        acc0 = sb("acc0", [128, 2, W])
        acc1 = sb("acc1", [128, 2, W])
        xo = sb("xo", [128, 2, W])

        pa = es.enter_context(nc.psum_tensor("pa", [128, 4, 512], F32))
        pb = es.enter_context(nc.psum_tensor("pb", [128, 2, 512], F32))
        pc = es.enter_context(nc.psum_tensor("pc", [128, 2, 512], F32))

        loaded = [signal(f"loaded{p}", 48) for p in range(2)]
        stored = [signal(f"stored{p}", 16) for p in range(2)]
        weights_in = signal("weights_in").sem
        made_pool = signal("made_pool").sem
        made_dve = signal("made_dve").sem
        made_pe = signal("made_pe").sem
        made_act = signal("made_act").sem
        a_bn = signal("a_bn")
        a_stats = signal("a_stats")
        a_ve = signal("a_ve")
        a_rstd = signal("a_rstd")
        a_xn = signal("a_xn")
        a_mask = signal("a_mask")
        a_endc = signal("a_endc")
        a_xT = signal("a_xT")
        a_cT = signal("a_cT")
        a_qT = signal("a_qT")
        a_kT = signal("a_kT")
        a_score = signal("a_score", 2)
        a_max = signal("a_max", 2)
        a_sub = signal("a_sub", 2)
        a_exp = signal("a_exp", 2)
        a_turn = signal("a_turn", 2)
        a_prT = signal("a_prT", 2)
        a_vx = signal("a_vx")
        a_pv = signal("a_pv")
        a_rden = signal("a_rden")
        a_att = signal("a_att")
        a_x1 = signal("a_x1")
        a_ss = signal("a_ss")
        a_ssm = signal("a_ssm")
        a_rk = signal("a_rk")
        a_hp0 = signal("a_hp0")
        a_hp = signal("a_hp")
        a_at = signal("a_at")
        a_cnt = signal("a_cnt")
        a_bm = signal("a_bm")
        a_cum = signal("a_cum")
        a_pick = signal("a_pick")
        a_scan = signal("a_scan")
        a_dep = signal("a_dep")
        b_bn = signal("b_bn")
        b_stats = signal("b_stats")
        b_ve = signal("b_ve")
        b_rstd = signal("b_rstd")
        b_xn = signal("b_xn")
        b_psum = signal("b_psum", 2 * FC + 2)
        b_hi = signal("b_hi", 2 * FC + 1)
        b_lo = signal("b_lo", 2 * FC + 1)
        b_x2 = signal("b_x2")
        c_bn = signal("c_bn", 2)
        c_stats = signal("c_stats", 2)
        c_ve = signal("c_ve", 2)
        c_rstd = signal("c_rstd", 2)
        c_xn = signal("c_xn", 2)
        c_turn = signal("c_turn", 2)
        c_yT = signal("c_yT", 2)
        c_proj = signal("c_proj")
        c_x3 = signal("c_x3")
        c_gate = signal("c_gate")
        c_gl = signal("c_gl")
        c_gm = signal("c_gm")
        c_gd = signal("c_gd")
        c_ge = signal("c_ge")
        c_gs = signal("c_gs")
        c_gr = signal("c_gr")
        c_gp = signal("c_gp")
        c_top = signal("c_top")
        c_topi = signal("c_topi")
        c_topf = signal("c_topf")
        c_hit = signal("c_hit")
        c_hitw = signal("c_hitw")
        c_wgt = signal("c_wgt")
        c_wT = signal("c_wT")
        c_wTs = signal("c_wTs")
        c_bias = signal("c_bias")
        c_acc0 = signal("c_acc0")
        c_moe = signal("c_moe", 2 * G)
        c_sum = signal("c_sum", E * G)
        c_out = signal("c_out")

        PAIRS = NG // 2 - 3

        def pipeline(eng, steps):
            def groups(it, i, last=NG - 1):
                return [Group(it - d, i) if 0 <= it - d <= last else None for d in range(5)]
            for it in range(6):
                steps(*groups(it, 0))
            with eng.Fori(0, PAIRS) as i:
                steps(*groups(6, i))
                steps(*groups(7, i))
            for it in range(NG, NG + 4):
                steps(*groups(it, 0))

        def bcast(ap, n):
            return ap.partition_broadcast(n)

        block = es.enter_context(nc.Block())

        @block.sync
        def _(sp):
            loads = [
                (lens_i[:], lens), (k0_u[:], k0.rearrange("(a p) f -> p a f", p=128)),
                (k1_u[:], k1.rearrange("(a p) f -> p a f", p=128)),
                (k2_u[:], k2.rearrange("(a p) f -> p a f", p=128)),
                (s_raw[:, 0:1], bcast(s0, 128)), (s_raw[:, 1:2], bcast(s1, 128)), (s_raw[:, 2:3], bcast(s2, 128)),
                (battn[:], bcast(b_attn, 128)),
                (nat[:, 0:E, :], w_moe.rearrange("e o d -> o e d")), (nat[:, E, :], w_in),
                (nat[0:E, E + 1, :], w_gate), (gres[:], g_res.rearrange("(d a) -> d a", a=1)),
                (bmoe[:], b_moe), (bgate[:], bcast(b_gate, 128)),
                (gpatch[:], bcast(g_init[0:D], NK)), (bin_b[:], bcast(b_in, NK)),
            ]
            assert len(loads) == WEIGHT_LOADS

            def load(g):
                if g.has(2):
                    sp.wait_ge(a_x1.sem, a_x1.of(g, back=2))
                    sp.wait_ge(a_vx.sem, a_vx.of(g, back=2))
                    sp.wait_ge(a_hp0.sem, a_hp0.of(g, back=2))
                    sp.wait_ge(a_mask.sem, a_mask.of(g, back=2))
                sp.dma_start(xa[:, g.p, :].rearrange("s (j d) -> s j d", j=G),
                             x[bass.ds(g.n * G, G)].rearrange("j s d -> s j d")).then_inc(loaded[g.p].sem, 16)
                sp.dma_start(cx[:, g.p], ctx[bass.ds(g.n * G, G)].rearrange("j k d -> k j d")).then_inc(loaded[g.p].sem, 16)
                sp.dma_start(mask_i[:, g.p, :],
                             mask[bass.ds(g.n * G, G)].rearrange("j k -> (j k)").partition_broadcast(128)
                             ).then_inc(loaded[g.p].sem, 16)

            def store(g):
                sp.wait_ge(c_out.sem, c_out.of(g))
                sp.dma_start(out[bass.ds(g.n * G, G)].rearrange("j s d -> s j d"),
                             xo[:, g.p, :].rearrange("s (j d) -> s j d", j=G)).then_inc(stored[g.p].sem, 16)

            load(Group(0, 0))
            for dst, src in loads:
                sp.dma_start(dst, src).then_inc(weights_in, 16)
            for n in range(1, 5):
                load(Group(n, 0))
            with sp.Fori(0, NG // 2 - 3) as i:
                store(Group(0, i))
                load(Group(5, i))
                store(Group(1, i))
                load(Group(6, i))
            store(Group(NG - 6, 0))
            load(Group(NG - 1, 0))
            for n in range(NG - 5, NG):
                store(Group(n, 0))
            for p in range(2):
                sp.wait_ge(stored[p].sem, 16 * (NG // 2))

        @block.gpsimd
        def _(pool):
            nc.gpsimd.memset(ident[:], 0.0)
            nc.gpsimd.memset(tri[:], 1.0)
            nc.gpsimd.memset(ones_bf[:], 1.0)
            nc.gpsimd.memset(neg_half[:], -0.5)
            nc.gpsimd.memset(spare_pool[:], 0.0)
            nc.gpsimd.memset(eps[:, :, 0], LN_EPS)
            nc.gpsimd.memset(eps[:, :, 1], RMS_EPS * LN_EPS / (1 + RMS_EPS))
            nc.gpsimd.memset(eps[:, :, 2], DC * RMS_EPS)
            nc.gpsimd.memset(vx[:], 1.0)
            nc.gpsimd.iota(step_i[:], [[1, S]], base=0, channel_multiplier=0)
            nc.gpsimd.iota(rank_i[:], [[0, 1]], base=1, channel_multiplier=1)
            nc.gpsimd.iota(lag_i[:], [[1, NK]], base=0, channel_multiplier=-1)
            nc.gpsimd.iota(expert_i[:], [[1, E]], base=0, channel_multiplier=0)
            nc.gpsimd.iota(row_i[:], [[0, 2]], base=0, channel_multiplier=1).then_inc(made_pool, 1)
            pool.wait_ge(made_pool, 1)
            nc.gpsimd.affine_select(out=ident[:], in_=ident[:], compare_op=ALU.not_equal, fill=1.0, base=0,
                                    pattern=[[-1, 128]], channel_multiplier=1)
            nc.gpsimd.affine_select(out=tri[:], in_=tri[:], compare_op=ALU.is_ge, fill=0.0, base=0,
                                    pattern=[[1, S]], channel_multiplier=-1)
            nc.gpsimd.tensor_copy(lag[:], lag_i[:]).then_inc(made_pool, 1)
            pool.wait_ge(made_pool, 2)
            nc.gpsimd.affine_select(out=lag2[:], in_=lag[:], compare_op=ALU.is_ge, fill=1e4, base=0,
                                    pattern=[[1, NK]], channel_multiplier=-1).then_inc(made_pool, 1)
            pool.wait_ge(weights_in, 16 * WEIGHT_LOADS)
            nc.gpsimd.tensor_scalar(gpatch[:], gpatch[:], GAIN, float(DC) ** 0.5, ALU.mult, ALU.mult).then_inc(made_pool, 1)
            pool.wait_ge(made_pool, 4)

            def rstd(n, g, stats, k, ve_sig, out_sig, k_eps=0):
                pool.wait_ge(stats.sem, stats.of(g, k))
                nc.gpsimd.tensor_tensor(ve[n][:], mv[n][:, :, 1], eps[:, :, k_eps], ALU.add).then_inc(ve_sig.sem, 1)
                pool.wait_ge(ve_sig.sem, ve_sig.of(g, k))
                nc.gpsimd.tensor_tensor(rs[n][:], ve[n][:], neg_half[:], ALU.pow).then_inc(out_sig.sem, 1)

            def patches(g):
                pool.wait_ge(loaded[g.p].sem, 48 * g.half + 48)
                if g.has(2):
                    pool.wait_ge(a_pv.sem, a_pv.of(g, back=2))
                nc.gpsimd.tensor_tensor(spare_pool[:, 0:1], spare_pool[:, 1:2], spare_pool[:, 2:3], ALU.add)
                nc.gpsimd.tensor_copy(vx[:, g.p, :, :, 0:HD],
                                      cx[:, g.p, :, D:2 * D].rearrange("k j (h d) -> k j h d", h=HEADS)
                                      ).then_inc(a_vx.sem, 1)
                pool.wait_ge(a_ss.sem, a_ss.of(g))
                nc.gpsimd.tensor_tensor(ssm[:], ss[:], eps[0:NK, :, 2], ALU.add).then_inc(a_ssm.sem, 1)
                pool.wait_ge(a_ssm.sem, a_ssm.of(g))
                nc.gpsimd.tensor_tensor(rk[:], ssm[:], neg_half[0:NK, :], ALU.pow).then_inc(a_rk.sem, 1)
                pool.wait_ge(a_rk.sem, a_rk.of(g))
                nc.gpsimd.tensor_tensor(hp0[:], cx[:, g.p, :, 0:D], rk[:].unsqueeze(2).to_broadcast([NK, G, D]),
                                        ALU.mult).then_inc(a_hp0.sem, 1)
                pool.wait_ge(a_hp0.sem, a_hp0.of(g))
                if g.has(1):
                    pool.wait_ge(a_scan.sem, a_scan.of(g, back=1))
                nc.gpsimd.tensor_tensor(hp[:], hp0[:], gpatch[:].unsqueeze(1).to_broadcast([NK, G, D]),
                                        ALU.mult).then_inc(a_hp.sem, 1)

            def boundaries(g):
                pool.wait_ge(a_endc.sem, a_endc.of(g))
                if g.has(1):
                    pool.wait_ge(a_cnt.sem, a_cnt.of(g, back=1))
                nc.gpsimd.tensor_tensor(spare_pool[:, 0:1], spare_pool[:, 1:2], spare_pool[:, 2:3], ALU.add)
                for j in range(G):
                    last = nc.gpsimd.tensor_scalar(at_end[:, j, :], step[:], endc[:, j:j + 1], None, ALU.is_equal)
                last.then_inc(a_at.sem, 1)

            def add_up(g):
                pool.wait_ge(c_sum.sem, c_sum.of(g))
                if g.has(2):
                    pool.wait_ge(stored[g.p].sem, 16 * g.half)
                nc.gpsimd.tensor_tensor(xo[:, g.p, :], acc0[:, g.p, :], acc1[:, g.p, :], ALU.add).then_inc(c_out.sem, 1)

            def steps(p, a, b, c, e):
                if b:
                    rstd(1, b, b_stats, 1, b_ve, b_rstd)
                if c:
                    rstd(2, c, c_stats, 1, c_ve, c_rstd, 1)
                if a:
                    boundaries(a)
                if p:
                    rstd(0, p, a_stats, 1, a_ve, a_rstd)
                if c:
                    rstd(3, c, c_stats, 2, c_ve, c_rstd)
                if p:
                    patches(p)
                if e:
                    add_up(e)

            pipeline(pool, steps)

        @block.vector
        def _(dve):
            dve.wait_ge(made_pool, 3)
            nc.vector.tensor_copy(step[:], step_i[:])
            nc.vector.tensor_copy(rank[:], rank_i[:])
            nc.vector.tensor_copy(expert[:], expert_i[:])
            nc.vector.tensor_scalar(row_i[:], row_i[:], HD, None, ALU.bitwise_and)
            nc.vector.memset(zero_b[:], 0.0).then_inc(made_dve, 1)
            dve.wait_ge(made_dve, 1)
            nc.vector.tensor_copy(row_f[:], row_i[:]).then_inc(made_dve, 1)
            dve.wait_ge(made_dve, 2)
            qs = float(HD) ** -0.5
            nc.vector.tensor_scalar(head_scale[:, 0:1], row_f[:, 0:1], -qs / HD, qs, ALU.mult, ALU.add)
            nc.vector.tensor_scalar(head_scale[:, 1:2], row_f[:, 1:2], qs / HD, None, ALU.mult)
            dve.wait_ge(weights_in, 16 * WEIGHT_LOADS)
            nc.vector.tensor_copy(lens_f[:], lens_i[:])
            nc.vector.tensor_scalar(s_sgn[:, 0:3], s_raw[:], 0.0, None, ALU.is_ge)
            nc.vector.tensor_tensor(k0_d[:], k0_u[:, 0, :], k0_u[:, 1, :], ALU.subtract).then_inc(made_dve, 1)
            dve.wait_ge(made_dve, 3)
            nc.vector.tensor_tensor_scan(ends[:], lens_f[:], zero_b[:], -1.0, ALU.add, ALU.add)
            nc.vector.tensor_scalar(s_sgn[:, 3:5], s_sgn[:, 0:2], 2.0, -1.0, ALU.mult, ALU.add).then_inc(made_dve, 1)
            dve.wait_ge(made_dve, 4)
            nc.vector.tensor_scalar(wrap[:], ends[:], 0.0, float(S), ALU.is_lt, ALU.mult)
            nc.vector.tensor_tensor(s_sgn[:, 0:2], s_sgn[:, 3:5], s_raw[:, 0:2], ALU.mult)
            nc.vector.tensor_scalar(s_sgn[:, 5:6], s_sgn[:, 4:5], 0.5, None, ALU.mult)
            nc.vector.tensor_scalar(s_sgn[:, 6:7], s_sgn[:, 4:5], -0.25, None, ALU.mult)
            nc.vector.tensor_scalar(s_sgn[:, 7:8], s_sgn[:, 3:4], 2.0, None, ALU.mult).then_inc(made_dve, 1)
            dve.wait_ge(made_dve, 5)
            nc.vector.tensor_tensor(ends[:], ends[:], wrap[:], ALU.add)
            nc.vector.scalar_tensor_tensor(s_sgn[:, 2:3], s_sgn[:, 0:1], s_sgn[:, 1:2], s_raw[:, 2:3], ALU.mult, ALU.mult)
            nc.vector.tensor_scalar(w1[:], k0_d[:], s_sgn[:, 7:8], None, ALU.mult)
            nc.vector.tensor_scalar(w2[:], k1_u[:], s_sgn[:, 5:6], s_sgn[:, 6:7], ALU.mult, ALU.add)
            nc.vector.tensor_scalar(w3[:], k2_u[:], 2.0, -1.0, ALU.mult, ALU.add).then_inc(made_dve, 1)
            dve.wait_ge(made_dve, 6)
            nc.vector.tensor_scalar(s_sgn[:, 2:3], s_sgn[:, 2:3], 16.0, None, ALU.mult).then_inc(made_dve, 1)
            dve.wait_ge(made_pe, 1)
            nc.vector.tensor_copy(w_moeT[:, 0:512], pa[:, 0, :])
            nc.vector.tensor_copy(w_moeT[:, 512:1024], pa[:, 1, :])
            nc.vector.tensor_scalar(w_inT[:], pa[:, 2, 0:D], gres[:, 0:1], (1 + RMS_EPS) ** -0.5, ALU.mult, ALU.mult)
            nc.vector.tensor_copy(w_gateT[:], pa[:, 2, D:D + E])
            nc.vector.tensor_copy(endsT[:], pa[0:NK, 3, 0:B]).then_inc(made_dve, 1)
            dve.wait_ge(made_dve, 8)

            def stats(n, src, g, k, bn, sig):
                for j in range(G):
                    last = nc.vector.bn_stats(st[n][:, j, :], src[:, j * D:(j + 1) * D])
                last.then_inc(bn.sem, 1)
                dve.wait_ge(bn.sem, bn.of(g, k))
                nc.vector.memset(spare_dve[:], 0.0)
                for j in range(G):
                    last = nc.vector.bn_aggr(mv[n][:, j, :], st[n][:, j, :])
                last.then_inc(sig.sem, 1)

            def normalise(n, src, g, k, rstd, sig):
                dve.wait_ge(rstd.sem, rstd.of(g, k))
                for j in range(G):
                    last = nc.vector.tensor_scalar(xn[n][:, j * D:(j + 1) * D], src[:, j * D:(j + 1) * D],
                                                   mv[n][:, j, 0:1], rs[n][:, j:j + 1], ALU.subtract, ALU.mult)
                last.then_inc(sig.sem, 1)

            def a_start(g):
                dve.wait_ge(loaded[g.p].sem, 48 * g.half + 48)
                stats(0, xa[:, g.p, :], g, 1, a_bn, a_stats)

            def a_masks(g):
                if g.has(1):
                    dve.wait_ge(a_score.sem, a_score.of(g, back=1))
                nc.vector.tensor_scalar(mask_b[:], mask_i[:, g.p, :], -1.0, -NEG, ALU.add, ALU.mult).then_inc(a_mask.sem, 1)

            def a_ends(g):
                if g.has(1):
                    dve.wait_ge(a_at.sem, a_at.of(g, back=1))
                nc.vector.tensor_copy(endc[:], endsT[:, bass.ds(g.n * G, G)]).then_inc(a_endc.sem, 1)

            def a_normalise(g):
                if g.has(1):
                    dve.wait_ge(a_xT.sem, a_xT.of(g, back=1))
                normalise(0, xa[:, g.p, :], g, 1, a_rstd, a_xn)

            def a_softmax(g, q):
                scores = pa[:, :, 0:2 * HR * NK].rearrange("p r (j e k) -> p r j e k", j=2, e=HR)
                dve.wait_ge(a_score.sem, a_score.of(g, q + 1))
                for j in range(2):
                    last = nc.vector.tensor_reduce(mx[:, q, j, :].rearrange("p (r e) -> p r e", r=R), scores[:, :, j], X, ALU.max)
                last.then_inc(a_max.sem, 1)
                dve.wait_ge(a_max.sem, a_max.of(g, q + 1))
                if g.has(1):
                    dve.wait_ge(a_turn.sem, a_turn.of(g, q + 1, back=1))
                for j in range(2):
                    last = nc.vector.tensor_tensor(
                        pr[:, q, :, j], scores[:, :, j],
                        mx[:, q, j, :].rearrange("p (r e) -> p r e", r=R).unsqueeze(3).to_broadcast([128, R, HR, NK]),
                        ALU.subtract)
                last.then_inc(a_sub.sem, 1)

            def a_boundary(g):
                dve.wait_ge(a_cnt.sem, a_cnt.of(g))
                nc.vector.tensor_scalar(bm[:], pa[:, 3, 0:G], 1.0, None, ALU.min).then_inc(a_bm.sem, 1)

            def a_depool(g):
                dve.wait_ge(a_scan.sem, a_scan.of(g))
                if g.has(2):
                    dve.wait_ge(c_proj.sem, c_proj.of(g, back=2))
                nc.vector.tensor_tensor(dep[:, g.p], pa[0:NK, 2, :].rearrange("k (j d) -> k j d", j=G),
                                        bin_b[:].unsqueeze(1).to_broadcast([NK, G, D]), ALU.add).then_inc(a_dep.sem, 1)
                dve.wait_ge(a_cum.sem, a_cum.of(g))
                nc.vector.tensor_scalar(pick[:, g.p], pa[0:NK, 3, :].rearrange("k (j s) -> k j s", j=G), 1.0, rank[:, 0:1],
                                        ALU.max, ALU.is_equal).then_inc(a_pick.sem, 1)

            def a_end(g):
                dve.wait_ge(a_pv.sem, a_pv.of(g))
                po = pa[:, 0:2, 0:2 * HEADS * (HD + 1)].rearrange("p b (j h c) -> p b j h c", j=2, h=HEADS)
                for b in range(2):
                    last = nc.vector.reciprocal(rden[:, 2 * b:2 * b + 2, :], po[:, b, :, :, HD])
                last.then_inc(a_rden.sem, 1)
                dve.wait_ge(a_rden.sem, a_rden.of(g))
                for j in range(G):
                    last = nc.vector.tensor_tensor(
                        att[:, j * D:(j + 1) * D].rearrange("p (h c) -> p h c", h=HEADS), po[:, j // 2, j % 2, :, 0:HD],
                        rden[:, j, :].unsqueeze(2).to_broadcast([128, HEADS, HD]), ALU.mult)
                last.then_inc(a_att.sem, 1)
                dve.wait_ge(a_att.sem, a_att.of(g))
                nc.vector.tensor_tensor(xb[:, g.p, :], att[:], xa[:, g.p, :], ALU.add).then_inc(a_x1.sem, 1)

            def b_start(g):
                dve.wait_ge(a_x1.sem, a_x1.of(g))
                stats(1, xb[:, g.p, :], g, 1, b_bn, b_stats)

            def b_normalise(g):
                if g.has(1):
                    dve.wait_ge(b_psum.sem, b_psum.of(g, 1, back=1))
                normalise(1, xb[:, g.p, :], g, 1, b_rstd, b_xn)

            def b_low(g, k):
                dve.wait_ge(b_hi.sem, b_hi.of(g, k + 1))
                src = pb[:, k % 2, :]
                if k == 0:
                    last = nc.vector.tensor_tensor(zT[:, 1, :], src, zT[:, 0, :], ALU.subtract)
                else:
                    h = h1 if k <= FC else h2
                    last = nc.vector.scalar_tensor_tensor(h[:, 1, (k - 1) % FC, :], src, 0.0, h[:, 0, (k - 1) % FC, :],
                                                          ALU.max, ALU.subtract)
                last.then_inc(b_lo.sem, 1)

            def b_end(g):
                k = 2 * FC + 1
                dve.wait_ge(b_psum.sem, b_psum.of(g, k + 1))
                nc.vector.scalar_tensor_tensor(xc[:, g.p, :], pb[:, k % 2, :], s_sgn[:, 2:3], xb[:, g.p, :],
                                               ALU.mult, ALU.add).then_inc(b_x2.sem, 1)

            def c_start(g):
                dve.wait_ge(b_x2.sem, b_x2.of(g))
                stats(2, xc[:, g.p, :], g, 1, c_bn, c_stats)

            def c_normalise(g, k):
                if g.has(1):
                    dve.wait_ge(c_turn.sem, c_turn.of(g, k, back=1))
                normalise(1 + k, xc[:, g.p, :] if k == 1 else xd[:], g, k, c_rstd, c_xn)

            def c_mid(g):
                dve.wait_ge(c_proj.sem, c_proj.of(g))
                nc.vector.tensor_tensor(xd[:], pc[:, 1, :], xc[:, g.p, :], ALU.add).then_inc(c_x3.sem, 1)
                dve.wait_ge(c_x3.sem, c_x3.of(g))
                stats(3, xd[:], g, 2, c_bn, c_stats)

            def c_gates(g):
                dve.wait_ge(c_gate.sem, c_gate.of(g))
                nc.vector.tensor_tensor(gl[:], pc[:, 1, 0:G * E].rearrange("p (j e) -> p j e", j=G),
                                        bgate[:].unsqueeze(1).to_broadcast([128, G, E]), ALU.add).then_inc(c_gl.sem, 1)
                dve.wait_ge(c_gl.sem, c_gl.of(g))
                nc.vector.tensor_reduce(gm[:], gl[:], X, ALU.max).then_inc(c_gm.sem, 1)
                dve.wait_ge(c_gm.sem, c_gm.of(g))
                nc.vector.tensor_tensor(gd[:], gl[:], gm[:].unsqueeze(2).to_broadcast([128, G, E]),
                                        ALU.subtract).then_inc(c_gd.sem, 1)

            def c_gates2(g):
                dve.wait_ge(c_ge.sem, c_ge.of(g))
                nc.vector.tensor_reduce(gs[:], ge[:], X, ALU.add).then_inc(c_gs.sem, 1)
                dve.wait_ge(c_gs.sem, c_gs.of(g))
                nc.vector.reciprocal(gr[:], gs[:]).then_inc(c_gr.sem, 1)
                dve.wait_ge(c_gr.sem, c_gr.of(g))
                nc.vector.tensor_tensor(gp[:], ge[:], gr[:].unsqueeze(2).to_broadcast([128, G, E]),
                                        ALU.mult).then_inc(c_gp.sem, 1)
                dve.wait_ge(c_gp.sem, c_gp.of(g))
                nc.vector.memset(spare_dve[:], 0.0)
                for j in range(G):
                    last = nc.vector.max(top[:, j, :], gp[:, j, :])
                last.then_inc(c_top.sem, 1)
                dve.wait_ge(c_top.sem, c_top.of(g))
                nc.vector.memset(spare_dve[:], 0.0)
                for j in range(G):
                    last = nc.vector.max_index(topi[:, j, :], top[:, j, :], gp[:, j, :])
                last.then_inc(c_topi.sem, 1)
                dve.wait_ge(c_topi.sem, c_topi.of(g))
                nc.vector.tensor_copy(topf[:], topi[:]).then_inc(c_topf.sem, 1)
                dve.wait_ge(c_topf.sem, c_topf.of(g))
                for t in range(2):
                    last = nc.vector.tensor_tensor(hit[:, t], expert[:].unsqueeze(1).to_broadcast([128, G, E]),
                                                   topf[:, :, t:t + 1].to_broadcast([128, G, E]), ALU.is_equal)
                last.then_inc(c_hit.sem, 1)
                dve.wait_ge(c_hit.sem, c_hit.of(g))
                for t in range(2):
                    last = nc.vector.tensor_tensor(hitw[:, t], hit[:, t], top[:, :, t:t + 1].to_broadcast([128, G, E]), ALU.mult)
                last.then_inc(c_hitw.sem, 1)
                dve.wait_ge(c_hitw.sem, c_hitw.of(g))
                nc.vector.tensor_tensor(wgt[:, g.p], hitw[:, 0], hitw[:, 1], ALU.add).then_inc(c_wgt.sem, 1)

            def c_bias_in(g):
                if g.has(2):
                    dve.wait_ge(c_out.sem, c_out.of(g, back=2))
                dve.wait_ge(c_bias.sem, c_bias.of(g))
                nc.vector.tensor_tensor(acc0[:, g.p], pc[:, 1, :], xd[:], ALU.add).then_inc(c_acc0.sem, 1)

            def c_experts(g, j, half):
                dve.wait_ge(c_moe.sem, c_moe.of(g, 2 * j + half + 1))
                if j == 0 and half == 0:
                    dve.wait_ge(c_acc0.sem, c_acc0.of(g))
                cols = slice(j * D, (j + 1) * D)
                for e in range(4 * half, 4 * half + 4):
                    src = pc[:, half, (e % 4) * D:(e % 4 + 1) * D]
                    w = wgt[:, g.p, j, e:e + 1]
                    acc = (acc1 if e % 2 else acc0)[:, g.p, :]
                    if e >= 2:
                        dve.wait_ge(c_sum.sem, c_sum.of(g, E * j + e - 1))
                    if e == 1:
                        last = nc.vector.tensor_scalar(acc[:, cols], src, w, None, ALU.mult)
                    else:
                        last = nc.vector.scalar_tensor_tensor(acc[:, cols], src, w, acc[:, cols], ALU.mult, ALU.add)
                    last.then_inc(c_sum.sem, 1)

            def steps(p, a, b, c, e):
                if b:
                    b_start(b)
                if c:
                    c_start(c)
                if a:
                    a_ends(a)
                    a_softmax(a, 0)
                if b:
                    b_normalise(b)
                if e:
                    c_experts(e, 0, 0)
                    c_experts(e, 0, 1)
                if c:
                    c_normalise(c, 1)
                if b:
                    b_low(b, 0)
                if a:
                    a_softmax(a, 1)
                if b:
                    b_low(b, 1)
                    b_low(b, 2)
                if e:
                    c_experts(e, 1, 0)
                if c:
                    c_mid(c)
                if b:
                    b_low(b, 3)
                if e:
                    c_experts(e, 1, 1)
                if p:
                    a_start(p)
                if b:
                    b_low(b, 4)
                if c:
                    c_normalise(c, 2)
                if b:
                    b_low(b, 5)
                if p:
                    a_masks(p)
                    a_normalise(p)
                if c:
                    c_gates(c)
                if e:
                    c_experts(e, 2, 0)
                if b:
                    b_low(b, 6)
                if c:
                    c_gates2(c)
                if e:
                    c_experts(e, 2, 1)
                if b:
                    b_low(b, 7)
                if a:
                    a_boundary(a)
                if b:
                    b_low(b, 8)
                if a:
                    a_depool(a)
                if c:
                    c_bias_in(c)
                if e:
                    c_experts(e, 3, 0)
                if b:
                    b_end(b)
                if e:
                    c_experts(e, 3, 1)
                if a:
                    a_end(a)

            pipeline(dve, steps)

        @block.scalar
        def _(act):
            act.wait_ge(made_pool, 3)
            nc.scalar.activation(decayT[:], lag2[:], ACT.Exp, scale=-float(DT)).then_inc(made_act, 1)
            act.wait_ge(made_dve, 8)

            def a_turned(g):
                act.wait_ge(a_xT.sem, a_xT.of(g))
                if g.has(1):
                    act.wait_ge(a_score.sem, a_score.of(g, back=1))
                nc.scalar.activation(qT[:], pa[:, 2, :], ACT.Copy).then_inc(a_qT.sem, 1)
                act.wait_ge(a_cT.sem, a_cT.of(g))
                for e in range(HR):
                    last = nc.scalar.activation(kT[:, e], pa[:, 3, 0:G * NK].rearrange("p (j k) -> p j k", j=G),
                                                ACT.Copy, scale=head_scale[:, e:e + 1])
                last.then_inc(a_kT.sem, 1)

            def a_squares(g):
                act.wait_ge(loaded[g.p].sem, 48 * g.half + 48)
                if g.has(1):
                    act.wait_ge(a_ssm.sem, a_ssm.of(g, back=1))
                for j in range(G):
                    last = nc.scalar.activation(sq[:, j, :], cx[:, g.p, j, :], ACT.Square, accum_out=ss[:, j:j + 1])
                last.then_inc(a_ss.sem, 1)

            def a_exponent(g, q):
                act.wait_ge(a_sub.sem, a_sub.of(g, q + 1))
                flat = pr[:, q].rearrange("p r j e k -> p (r j e k)")
                nc.scalar.activation(flat, flat, ACT.Exp).then_inc(a_exp.sem, 1)

            def a_turned_back(g, q):
                act.wait_ge(a_turn.sem, a_turn.of(g, q + 1))
                if g.has(1):
                    act.wait_ge(a_pv.sem, a_pv.of(g, back=1))
                for j in range(2):
                    last = nc.scalar.activation(prT[:, 2 * q + j].rearrange("k (b h) s -> k b (h s)", b=2),
                                                pa[0:NK, 2 * j:2 * j + 2, :], ACT.Copy)
                last.then_inc(a_prT.sem, 1)

            def b_high(g, k):
                act.wait_ge(b_psum.sem, b_psum.of(g, k + 1))
                src = pb[:, k % 2, :]
                if k == 0:
                    if g.has(1):
                        act.wait_ge(b_psum.sem, b_psum.of(g, 1 + FC, back=1))
                    last = nc.scalar.activation(zT[:, 0, :], src, ACT.Copy)
                else:
                    h = h1 if k <= FC else h2
                    last = nc.scalar.activation(h[:, 0, (k - 1) % FC, :], src, ACT.Relu)
                last.then_inc(b_hi.sem, 1)

            def c_turned(g, k):
                act.wait_ge(c_turn.sem, c_turn.of(g, k))
                if k == 1:
                    if g.has(1):
                        act.wait_ge(c_proj.sem, c_proj.of(g, back=1))
                    nc.scalar.activation(y3T[:], pc[:, 0, :], ACT.Copy).then_inc(c_yT.sem, 1)
                else:
                    if g.has(2):
                        act.wait_ge(c_moe.sem, c_moe.of(g, back=2))
                    nc.scalar.activation(y4T[:, g.p], pc[:, 0, :], ACT.Copy).then_inc(c_yT.sem, 1)

            def c_gate_exp(g):
                act.wait_ge(c_gd.sem, c_gd.of(g))
                nc.scalar.activation(ge[:], gd[:], ACT.Exp).then_inc(c_ge.sem, 1)

            def c_weights_turned(g):
                act.wait_ge(c_wT.sem, c_wT.of(g))
                nc.scalar.activation(wT[:], pc[0:E, 0, :], ACT.Copy).then_inc(c_wTs.sem, 1)

            def steps(p, a, b, c, e):
                if b:
                    b_high(b, 0)
                if a:
                    a_exponent(a, 0)
                if c:
                    c_turned(c, 1)
                if b:
                    b_high(b, 1)
                if a:
                    a_exponent(a, 1)
                if b:
                    b_high(b, 2)
                    b_high(b, 3)
                if a:
                    a_turned_back(a, 0)
                if b:
                    b_high(b, 4)
                if c:
                    c_turned(c, 2)
                if p:
                    a_squares(p)
                if a:
                    a_turned_back(a, 1)
                if b:
                    b_high(b, 5)
                if c:
                    c_gate_exp(c)
                if b:
                    b_high(b, 6)
                if p:
                    a_turned(p)
                if b:
                    b_high(b, 7)
                if c:
                    c_weights_turned(c)
                if b:
                    b_high(b, 8)

            pipeline(act, steps)

        @block.tensor
        def _(pe):
            pe.wait_ge(made_pool, 2 + 1)
            pe.wait_ge(weights_in, 16 * WEIGHT_LOADS)
            for e in range(E):
                pe.transpose(pa[:, e // 4, (e % 4) * D:(e % 4 + 1) * D], nat[:, e, :], ident[:])
            pe.transpose(pa[:, 2, 0:D], nat[:, E, :], ident[:])
            pe.transpose(pa[:, 2, D:D + E], nat[0:E, E + 1, :], ident[0:E, 0:E])
            pe.wait_ge(made_dve, 6)
            pe.transpose(pa[0:NK, 3, 0:B], ends[:], ident[0:B, 0:B]).then_inc(made_pe, 1)
            pe.wait_ge(made_dve, 8)
            pe.wait_ge(made_act, 1)
            pe.wait_ge(made_pool, 4)

            def turn4(dst, src, rows=128):
                for j in range(G):
                    last = pe.transpose(dst[:, j * rows:(j + 1) * rows], src(j), ident[0:rows, 0:rows])
                return last

            def a_turns(g):
                if g.has(1):
                    pe.wait_ge(a_prT.sem, a_prT.of(g, back=1))
                pe.wait_ge(loaded[g.p].sem, 48 * g.half + 48)
                turn4(pa[:, 3, :], lambda j: cx[:, g.p, j, 0:D], NK).then_inc(a_cT.sem, 1)
                pe.wait_ge(a_xn.sem, a_xn.of(g))
                turn4(pa[:, 2, :], lambda j: xn[0][:, j * D:(j + 1) * D]).then_inc(a_xT.sem, 1)

            def a_scores(g, q):
                if q == 0:
                    pe.wait_ge(a_qT.sem, a_qT.of(g))
                    pe.wait_ge(a_kT.sem, a_kT.of(g))
                    pe.wait_ge(a_mask.sem, a_mask.of(g))
                    if g.has(1):
                        pe.wait_ge(a_dep.sem, a_dep.of(g, back=1))
                        pe.wait_ge(a_pick.sem, a_pick.of(g, back=1))
                        pe.wait_ge(a_att.sem, a_att.of(g, back=1))
                else:
                    pe.wait_ge(a_sub.sem, a_sub.of(g, q))
                n = HR * NK
                for r in range(R):
                    rows = slice(32 * r, 32 * r + 32)
                    row = slice(32 * r, 32 * r + 1)
                    pe.matmul(pa[:, r, 0:2 * n], ones_bf[row, :],
                              mask_b[row, 2 * q * NK:(2 * q + 2) * NK].rearrange("o (j k) -> o j k", j=2)
                              .unsqueeze(2).to_broadcast([1, 2, HR, NK]), start=True, stop=False)
                for j in range(2):
                    for r in range(R):
                        rows = slice(32 * r, 32 * r + 32)
                        b = 2 * q + j
                        last = pe.matmul(pa[:, r, j * n:(j + 1) * n], qT[rows, b * S:(b + 1) * S], kT[rows, :, b, :],
                                         start=False, stop=(j == 1))
                last.then_inc(a_score.sem, 1)

            def a_turn_back(g, q):
                if q == 0:
                    pe.wait_ge(a_sub.sem, a_sub.of(g, 2))
                else:
                    pe.wait_ge(a_prT.sem, a_prT.of(g, 1))
                pe.wait_ge(a_exp.sem, a_exp.of(g, q + 1))
                for j in range(2):
                    for h in range(HEADS):
                        last = pe.transpose(pa[0:NK, 2 * j + h // 4, (h % 4) * S:(h % 4 + 1) * S],
                                            pr[:, q, h // HR, j, h % HR, :], ident[:])
                last.then_inc(a_turn.sem, 1)

            def a_values(g, j):
                if j == 0:
                    pe.wait_ge(a_prT.sem, a_prT.of(g, 2))
                    pe.wait_ge(a_vx.sem, a_vx.of(g))
                for h in range(HEADS):
                    at = ((j % 2) * HEADS + h) * (HD + 1)
                    last = pe.matmul(pa[:, j // 2, at:at + HD + 1], prT[:, j, h, :], vx[:, g.p, j, h, :],
                                     start=True, stop=True)
                if j == G - 1:
                    last.then_inc(a_pv.sem, 1)

            def a_count(g, p):
                pe.wait_ge(a_prT.sem, a_prT.of(g, 2))
                if p:
                    pe.wait_ge(a_qT.sem, a_qT.of(p))
                    pe.wait_ge(a_kT.sem, a_kT.of(p))
                pe.wait_ge(a_at.sem, a_at.of(g))
                for j in range(G):
                    last = pe.matmul(pa[:, 3, j:j + 1], at_end[:, j, :], ones_bf[0:NK, 0:1], start=True, stop=True)
                last.then_inc(a_cnt.sem, 1)
                pe.wait_ge(a_hp.sem, a_hp.of(g))
                pe.matmul(pa[0:NK, 2, :], decayT[:], hp[:].rearrange("k j d -> k (j d)"), start=True, stop=True
                          ).then_inc(a_scan.sem, 1)

            def a_cumulate(g):
                pe.wait_ge(a_bm.sem, a_bm.of(g))
                for j in range(G):
                    last = pe.matmul(pa[0:NK, 3, j * S:(j + 1) * S], bm[:, j:j + 1].to_broadcast([S, NK]), tri[:],
                                     start=True, stop=True)
                last.then_inc(a_cum.sem, 1)

            def b_turns(g):
                pe.wait_ge(b_xn.sem, b_xn.of(g))
                if g.has(1):
                    pe.wait_ge(b_lo.sem, b_lo.of(g, back=1))
                turn4(pb[:, 0, :], lambda j: xn[1][:, j * D:(j + 1) * D]).then_inc(b_psum.sem, 1)

            def b_layer(g, k):
                c = (k - 1) % FC
                if k >= 2:
                    pe.wait_ge(b_lo.sem, b_lo.of(g, k - 1))
                elif g.has(1):
                    pe.wait_ge(b_x2.sem, b_x2.of(g, back=1))
                if k <= FC:
                    pe.wait_ge(b_lo.sem, b_lo.of(g, 1))
                    for part in range(2):
                        last = pe.matmul(pb[:, k % 2, :], w1[:, c * 128:(c + 1) * 128], zT[:, part, :],
                                         start=(part == 0), stop=(part == 1))
                else:
                    for i in range(FC):
                        if k == FC + 1:
                            pe.wait_ge(b_lo.sem, b_lo.of(g, 2 + i))
                        for part in range(2):
                            last = pe.matmul(pb[:, k % 2, :], w2[:, i, c * 128:(c + 1) * 128], h1[:, part, i, :],
                                             start=(i == 0 and part == 0), stop=(i == FC - 1 and part == 1))
                last.then_inc(b_psum.sem, 1)

            def b_last(g):
                k = 2 * FC + 1
                pe.wait_ge(b_lo.sem, b_lo.of(g))
                for j in range(G):
                    for i in range(FC):
                        for part in range(2):
                            last = pe.matmul(pb[:, k % 2, j * D:(j + 1) * D], h2[:, part, i, j * S:(j + 1) * S], w3[:, i, :],
                                             start=(i == 0 and part == 0), stop=(i == FC - 1 and part == 1))
                last.then_inc(b_psum.sem, 1)

            def expert_bank_read(e, j, half):
                if e:
                    pe.wait_ge(c_sum.sem, c_sum.of(e, E * j + 4 * (half + 1)))

            def c_turns(g, k, e):
                pe.wait_ge(c_xn.sem, c_xn.of(g, k))
                expert_bank_read(e, k - 1, 0)
                if k == 1 and g.has(1):
                    pe.wait_ge(c_acc0.sem, c_acc0.of(g, back=1))
                turn4(pc[:, 0, :], lambda j: xn[1 + k][:, j * D:(j + 1) * D]).then_inc(c_turn.sem, 1)

            def c_project(g, e):
                pe.wait_ge(c_yT.sem, c_yT.of(g, 1))
                pe.wait_ge(a_dep.sem, a_dep.of(g))
                pe.wait_ge(a_pick.sem, a_pick.of(g))
                expert_bank_read(e, 0, 1)
                for j in range(G):
                    cols = slice(j * S, (j + 1) * S)
                    pe.matmul(pc[:, 1, cols], y3T[:, cols], w_inT[:], start=True, stop=False)
                    last = pe.matmul(pc[:, 1, cols], pick[:, g.p, j, :], dep[:, g.p, j, :], start=False, stop=True)
                last.then_inc(c_proj.sem, 1)

            def c_gate_scores(g, e):
                pe.wait_ge(c_yT.sem, c_yT.of(g, 2))
                expert_bank_read(e, 1, 1)
                for j in range(G):
                    last = pe.matmul(pc[:, 1, j * E:(j + 1) * E], y4T[:, g.p, j * S:(j + 1) * S], w_gateT[:],
                                     start=True, stop=True)
                last.then_inc(c_gate.sem, 1)

            def c_weight_turns(g, e):
                pe.wait_ge(c_wgt.sem, c_wgt.of(g))
                expert_bank_read(e, 2, 0)
                for j in range(G):
                    last = pe.transpose(pc[0:E, 0, j * S:(j + 1) * S], wgt[:, g.p, j, :], ident[:])
                last.then_inc(c_wT.sem, 1)

            def c_biases(g, e):
                pe.wait_ge(c_wTs.sem, c_wTs.of(g))
                expert_bank_read(e, 2, 1)
                for j in range(G):
                    last = pe.matmul(pc[:, 1, j * D:(j + 1) * D], wT[:, j * S:(j + 1) * S], bmoe[:], start=True, stop=True)
                last.then_inc(c_bias.sem, 1)

            def c_experts(g, j, half, c):
                if j == 0:
                    pe.wait_ge(c_acc0.sem, c_acc0.of(g))
                    if g.has(1):
                        pe.wait_ge(c_sum.sem, c_sum.of(g, back=1))
                elif c is None:
                    expert_bank_read(g, j - 1, half)
                elif half == 0:
                    after = {1: c_yT.of(c, 1), 2: c_yT.of(c, 2), 3: c_wTs.of(c)}[j]
                    pe.wait_ge((c_wTs if j == 3 else c_yT).sem, after)
                else:
                    after = {1: c_x3, 2: c_gl, 3: c_acc0}[j]
                    pe.wait_ge(after.sem, after.of(c))
                pe.matmul(pc[:, half, :], y4T[:, g.p, j * S:(j + 1) * S], w_moeT[:, half * 512:(half + 1) * 512],
                          start=True, stop=True).then_inc(c_moe.sem, 1)

            def steps(p, a, b, c, e):
                if a:
                    a_scores(a, 0)
                if e:
                    c_experts(e, 0, 0, c)
                    c_experts(e, 0, 1, c)
                if b:
                    b_turns(b)
                if a:
                    a_scores(a, 1)
                if c:
                    c_turns(c, 1, e)
                if b:
                    b_layer(b, 1)
                    b_layer(b, 2)
                if c:
                    c_project(c, e)
                if e:
                    c_experts(e, 1, 0, c)
                if b:
                    b_layer(b, 3)
                if a:
                    a_turn_back(a, 0)
                if e:
                    c_experts(e, 1, 1, c)
                if b:
                    b_layer(b, 4)
                if c:
                    c_turns(c, 2, e)
                if b:
                    b_layer(b, 5)
                if a:
                    a_turn_back(a, 1)
                if c:
                    c_gate_scores(c, e)
                if e:
                    c_experts(e, 2, 0, c)
                if p:
                    a_turns(p)
                if b:
                    b_layer(b, 6)
                if e:
                    c_experts(e, 2, 1, c)
                if a:
                    a_values(a, 0)
                    a_values(a, 1)
                if a:
                    a_count(a, p)
                if b:
                    b_layer(b, 7)
                if c:
                    c_weight_turns(c, e)
                if a:
                    a_values(a, 2)
                    a_values(a, 3)
                if b:
                    b_layer(b, 8)
                if a:
                    a_cumulate(a)
                if c:
                    c_biases(c, e)
                if e:
                    c_experts(e, 3, 0, c)
                if b:
                    b_last(b)
                if e:
                    c_experts(e, 3, 1, c)

            pipeline(pe, steps)


WEIGHT_LOADS = 16

_INS = ['x', 'ctx_2048', 'mask_BxS2_ik0', 'mask_BxS2_if0', 'L0_xattn_b', 'L0_ffn_k0', 'L0_ffn_k1', 'L0_ffn_k2',
        'L0_ffn_s0', 'L0_ffn_s1', 'L0_ffn_s2', 'L1_xattn_W_in', 'L1_xattn_b_in', 'L1_xattn_g_res', 'L1_xattn_g_init',
        'L1_ffn_W', 'L1_ffn_b', 'L1_ffn_Wg', 'L1_ffn_bg']


def kernel(**inputs):
    from concourse import bacc
    from concourse.bass_utils import run_bass_kernel_spmd

    nc = bacc.Bacc("TRN2", target_bir_lowering=False, num_devices=1)
    arrays, args = {}, []
    for name in _INS:
        a = np.ascontiguousarray(inputs[name])
        if a.ndim == 0:
            a = a.reshape(1)
        arrays[f"in_{name}"] = a
        args.append(nc.dram_tensor(f"in_{name}", a.shape, mybir.dt.from_np(a.dtype), kind="ExternalInput").ap())
    out = nc.dram_tensor("out_x", inputs['x'].shape, F32, kind="ExternalOutput").ap()
    build(nc, *args, out)
    r = run_bass_kernel_spmd(nc, [arrays], core_ids=[0])
    return r.results[0]["out_x"]
```
